# Optimizing a Trainium2 kernel written in Bass

```python
import numpy as np
import jax
import jax.numpy as jnp

def _softmax(x, axis=-1):
    return jax.nn.softmax(x, axis=axis)

def _gelu(x):
    return jax.nn.gelu(x, approximate=True)

def _silu(x):
    return jax.nn.silu(x)

def _sigmoid(x):
    return jax.nn.sigmoid(x)

def _layernorm(x, axis=-1, eps=1e-05):
    m = jnp.mean(x, axis=axis, keepdims=True)
    v = jnp.var(x, axis=axis, keepdims=True)
    return (x - m) / jnp.sqrt(v + eps)

def _scatter_add(tgt, idx, src, axis=0):
    return tgt.at[idx].add(src)

def _segment_sum(src, seg, n):
    return jax.ops.segment_sum(src, seg, n)
kernel_name = 'mk_pixart_resid_d1_seqx_r4_dd5409'

def setup_inputs(seed: int=0):
    np.random.seed(seed)
    _w = jnp.asarray

    def _rec_inputs():
        import jax
        import jax.numpy as jnp
        _rk = jax.random.key(seed)
        x = -0.003379 + 0.9984 * jax.random.normal(jax.random.fold_in(_rk, 1), (8, 256, 256), jnp.float32)
        _lenS = 256 - jax.random.randint(jax.random.fold_in(_rk, 7), (8,), 0, max(1, 256 // 4) + 1, jnp.int32)
        _lenS2 = 256 - jax.random.randint(jax.random.fold_in(_rk, 8), (8,), 0, max(1, 256 // 4) + 1, jnp.int32)
        cond_1024 = -0.0142567 + 1.00875 * jax.random.normal(jax.random.fold_in(_rk, 11), (8, 256), jnp.float32)
        _ctx_1024P = jax.random.normal(jax.random.fold_in(_rk, 12), (8, 16, 256), jnp.float32)
        _ctx_1024c = jax.random.dirichlet(jax.random.fold_in(_rk, 512), 0.3 * jnp.ones((16,), jnp.float32), (8, 256))
        _ctx_1024t = jnp.einsum('bsk,bkd->bsd', _ctx_1024c, _ctx_1024P)
        _ctx_1024t = _ctx_1024t * jax.lax.rsqrt(jnp.mean(jnp.square(_ctx_1024t)) + 1e-12) * 0.953939
        ctx_1024 = -5.72187e-05 + 0.999849 * (_ctx_1024t + 0.3 * jax.random.normal(jax.random.fold_in(_rk, 612), (8, 256, 256), jnp.float32))
        return (x, cond_1024, ctx_1024)
    x, cond_1024, ctx_1024 = _rec_inputs()

    def _L0_xcond_setup():
        import jax, jax.numpy as jnp
        import numpy as np
        B, N, K, D, T = (16, 1024, 16, 256, 3)
        EPS_ATTN = 1e-08
        LN_EPS = 1e-05

        def _ln(x, g, b):
            mu = jnp.mean(x, axis=-1, keepdims=True)
            var = jnp.mean(jnp.square(x - mu), axis=-1, keepdims=True)
            return (x - mu) * jax.lax.rsqrt(var + LN_EPS) * g + b
        key = jax.random.key(seed)
        ks = jax.random.split(key, 16)
        w = lambda k, i, o: jax.random.normal(k, (i, o), jnp.float32) * 0.02
        inp = {'x_cls': jax.random.normal(ks[0], (B, D), jnp.float32), 'x': jax.random.normal(ks[1], (B, N, D), jnp.float32), 'noise': jax.random.normal(ks[2], (B, K, D), jnp.float32), 'q_mu': jax.random.normal(ks[3], (1, 1, D), jnp.float32), 'q_logsig': jax.random.normal(ks[4], (1, 1, D), jnp.float32) * 0.02, 'lnkv_g': jnp.ones((D,), jnp.float32), 'lnkv_b': jnp.zeros((D,), jnp.float32), 'lnq_g': jnp.ones((D,), jnp.float32), 'lnq_b': jnp.zeros((D,), jnp.float32), 'lnm_g': jnp.ones((D,), jnp.float32), 'lnm_b': jnp.zeros((D,), jnp.float32), 'lnp_g': jnp.ones((D,), jnp.float32), 'lnp_b': jnp.zeros((D,), jnp.float32), 'wk': w(ks[5], D, D), 'bk': jnp.zeros((D,), jnp.float32), 'wv': w(ks[6], D, D), 'bv': jnp.zeros((D,), jnp.float32), 'wq': w(ks[7], D, D), 'bq': jnp.zeros((D,), jnp.float32), 'wu': w(ks[8], D, D), 'bu': jnp.zeros((D,), jnp.float32), 'w1': w(ks[9], D, D), 'b1': jnp.zeros((D,), jnp.float32), 'w2': w(ks[10], D, D), 'b2': jnp.zeros((D,), jnp.float32)}
        return inp
    _L0_xcond_all = _L0_xcond_setup()
    _L0_xcond_in = {k: v for k, v in _L0_xcond_all.items() if k in ('q_mu', 'q_logsig', 'lnkv_g', 'lnkv_b', 'lnq_g', 'lnq_b', 'lnm_g', 'lnm_b', 'lnp_g', 'lnp_b', 'wk', 'bk', 'wv', 'bv', 'wq', 'bq', 'wu', 'bu', 'w1', 'b1', 'w2', 'b2')}
    del _L0_xcond_all

    def _L0_ffn_setup():
        import jax, jax.numpy as jnp
        import numpy as np
        EPS = 1e-06
        LN_EPS = 1e-05

        def _absmean_core(W):
            gamma = jnp.mean(jnp.abs(W)) + EPS
            Ws = W / gamma
            Wq = jnp.sign(Ws) * jnp.minimum(jnp.round(jnp.abs(Ws)), 1.0)
            return (Wq, gamma)

        @jax.custom_vjp
        def absmean(W):
            return _absmean_core(W)[0]

        def _absmean_fwd(W):
            Wq, gamma = _absmean_core(W)
            return (Wq, gamma)

        def _absmean_bwd(gamma, g):
            return (g / gamma,)
        absmean.defvjp(_absmean_fwd, _absmean_bwd)

        def layernorm(x, w, b, eps=LN_EPS):
            mu = jnp.mean(x, axis=-1, keepdims=True)
            var = jnp.mean((x - mu) ** 2, axis=-1, keepdims=True)
            return (x - mu) * jax.lax.rsqrt(var + eps) * w + b
        key = jax.random.key(seed)
        k1, k2, k3 = jax.random.split(key, 3)
        d, h = (256, 1024)
        B, T = (8, 512)
        return {'x': jax.random.normal(k1, (B, T, d), jnp.float32), 'W_fc': jax.random.normal(k2, (h, d), jnp.float32), 'ln_w': jnp.ones((h,), jnp.float32), 'ln_b': jnp.zeros((h,), jnp.float32), 'W_proj': jax.random.normal(k3, (d, h), jnp.float32)}
    _L0_ffn_all = _L0_ffn_setup()
    _L0_ffn_in = {k: v for k, v in _L0_ffn_all.items() if k in ('W_fc', 'ln_w', 'ln_b', 'W_proj')}
    del _L0_ffn_all
    return {'x': x, 'cond_1024': cond_1024, 'ctx_1024': ctx_1024, 'L0_xcond_q_mu': _L0_xcond_in['q_mu'], 'L0_xcond_q_logsig': _L0_xcond_in['q_logsig'], 'L0_xcond_lnkv_g': _L0_xcond_in['lnkv_g'], 'L0_xcond_lnkv_b': _L0_xcond_in['lnkv_b'], 'L0_xcond_lnq_g': _L0_xcond_in['lnq_g'], 'L0_xcond_lnq_b': _L0_xcond_in['lnq_b'], 'L0_xcond_lnm_g': _L0_xcond_in['lnm_g'], 'L0_xcond_lnm_b': _L0_xcond_in['lnm_b'], 'L0_xcond_lnp_g': _L0_xcond_in['lnp_g'], 'L0_xcond_lnp_b': _L0_xcond_in['lnp_b'], 'L0_xcond_wk': _L0_xcond_in['wk'], 'L0_xcond_bk': _L0_xcond_in['bk'], 'L0_xcond_wv': _L0_xcond_in['wv'], 'L0_xcond_bv': _L0_xcond_in['bv'], 'L0_xcond_wq': _L0_xcond_in['wq'], 'L0_xcond_bq': _L0_xcond_in['bq'], 'L0_xcond_wu': _L0_xcond_in['wu'], 'L0_xcond_bu': _L0_xcond_in['bu'], 'L0_xcond_w1': _L0_xcond_in['w1'], 'L0_xcond_b1': _L0_xcond_in['b1'], 'L0_xcond_w2': _L0_xcond_in['w2'], 'L0_xcond_b2': _L0_xcond_in['b2'], 'L0_ffn_W_fc': _L0_ffn_in['W_fc'], 'L0_ffn_ln_w': _L0_ffn_in['ln_w'], 'L0_ffn_ln_b': _L0_ffn_in['ln_b'], 'L0_ffn_W_proj': _L0_ffn_in['W_proj']}

def reference(x, cond_1024, ctx_1024, L0_xcond_q_mu, L0_xcond_q_logsig, L0_xcond_lnkv_g, L0_xcond_lnkv_b, L0_xcond_lnq_g, L0_xcond_lnq_b, L0_xcond_lnm_g, L0_xcond_lnm_b, L0_xcond_lnp_g, L0_xcond_lnp_b, L0_xcond_wk, L0_xcond_bk, L0_xcond_wv, L0_xcond_bv, L0_xcond_wq, L0_xcond_bq, L0_xcond_wu, L0_xcond_bu, L0_xcond_w1, L0_xcond_b1, L0_xcond_w2, L0_xcond_b2, L0_ffn_W_fc, L0_ffn_ln_w, L0_ffn_ln_b, L0_ffn_W_proj):
    import jax
    import jax.numpy as jnp

    def _L0_xcond_ref(x_cls, x, noise, q_mu, q_logsig, lnkv_g, lnkv_b, lnq_g, lnq_b, lnm_g, lnm_b, lnp_g, lnp_b, wk, bk, wv, bv, wq, bq, wu, bu, w1, b1, w2, b2):
        import jax, jax.numpy as jnp
        import numpy as np
        B, N, K, D, T = (16, 1024, 16, 256, 3)
        EPS_ATTN = 1e-08
        LN_EPS = 1e-05

        def _ln(x, g, b):
            mu = jnp.mean(x, axis=-1, keepdims=True)
            var = jnp.mean(jnp.square(x - mu), axis=-1, keepdims=True)
            return (x - mu) * jax.lax.rsqrt(var + LN_EPS) * g + b
        scale = D ** (-0.5)
        x_in = _ln(x, lnkv_g, lnkv_b)
        k = x_in @ wk + bk
        v = x_in @ wv + bv
        slots = q_mu + jnp.exp(q_logsig) * noise
        for _ in range(T):
            prev = slots
            q = _ln(slots, lnq_g, lnq_b) @ wq + bq
            logits = jnp.einsum('bnd,bkd->bnk', k, q) / scale
            attn = jax.nn.softmax(logits, axis=-1) + EPS_ATTN
            attn = attn / jnp.sum(attn, axis=1, keepdims=True)
            upd = jnp.einsum('bnk,bnd->bkd', attn, v)
            slots = upd @ wu + bu + prev
            h = _ln(slots, lnm_g, lnm_b) @ w1 + b1
            slots = jax.nn.gelu(h, approximate=False) @ w2 + b2 + slots
            slots = _ln(slots + x_cls[:, None, :], lnp_g, lnp_b)
        return slots

    def _L0_ffn_ref(x, W_fc, ln_w, ln_b, W_proj):
        import jax, jax.numpy as jnp
        import numpy as np
        EPS = 1e-06
        LN_EPS = 1e-05

        def _absmean_core(W):
            gamma = jnp.mean(jnp.abs(W)) + EPS
            Ws = W / gamma
            Wq = jnp.sign(Ws) * jnp.minimum(jnp.round(jnp.abs(Ws)), 1.0)
            return (Wq, gamma)

        @jax.custom_vjp
        def absmean(W):
            return _absmean_core(W)[0]

        def _absmean_fwd(W):
            Wq, gamma = _absmean_core(W)
            return (Wq, gamma)

        def _absmean_bwd(gamma, g):
            return (g / gamma,)
        absmean.defvjp(_absmean_fwd, _absmean_bwd)

        def layernorm(x, w, b, eps=LN_EPS):
            mu = jnp.mean(x, axis=-1, keepdims=True)
            var = jnp.mean((x - mu) ** 2, axis=-1, keepdims=True)
            return (x - mu) * jax.lax.rsqrt(var + eps) * w + b
        h = jnp.einsum('btd,hd->bth', x, absmean(W_fc))
        h = jax.nn.gelu(h, approximate=False)
        h = layernorm(h, ln_w, ln_b)
        return jnp.einsum('bth,dh->btd', h, absmean(W_proj))
    x = x + _L0_xcond_ref(cond_1024, ctx_1024, _layernorm(x, axis=-1), L0_xcond_q_mu, L0_xcond_q_logsig, L0_xcond_lnkv_g, L0_xcond_lnkv_b, L0_xcond_lnq_g, L0_xcond_lnq_b, L0_xcond_lnm_g, L0_xcond_lnm_b, L0_xcond_lnp_g, L0_xcond_lnp_b, L0_xcond_wk, L0_xcond_bk, L0_xcond_wv, L0_xcond_bv, L0_xcond_wq, L0_xcond_bq, L0_xcond_wu, L0_xcond_bu, L0_xcond_w1, L0_xcond_b1, L0_xcond_w2, L0_xcond_b2)
    x = x + _L0_ffn_ref(_layernorm(x, axis=-1), L0_ffn_W_fc, L0_ffn_ln_w, L0_ffn_ln_b, L0_ffn_W_proj)
    return x

_drawn_inputs = setup_inputs


def setup_inputs(seed=0):
    import zlib

    import numpy as np

    out = dict(_drawn_inputs(seed))
    spreads = {'L0_xcond_lnkv_g': (1.0, 0.6),
     'L0_xcond_lnkv_b': (0.0, 0.729),
     'L0_xcond_lnq_g': (1.0, 0.6),
     'L0_xcond_lnq_b': (0.0, 0.8),
     'L0_xcond_lnm_g': (1.0, 0.6),
     'L0_xcond_lnm_b': (0.0, 0.8),
     'L0_xcond_lnp_g': (1.0, 0.2),
     'L0_xcond_lnp_b': (0.0, 0.1),
     'L0_xcond_bk': (0.0, 0.337),
     'L0_xcond_bv': (0.0, 0.321),
     'L0_xcond_bq': (0.0, 0.8),
     'L0_xcond_bu': (0.0, 0.1),
     'L0_xcond_b1': (0.0, 0.621),
     'L0_xcond_b2': (0.0, 0.1),
     'L0_ffn_ln_w': (1.0, 0.2),
     'L0_ffn_ln_b': (0.0, 0.1)}
    factors = {'L0_xcond_q_logsig': 8.0}
    for name, (base, spread) in spreads.items():
        noise = np.random.default_rng([zlib.crc32(name.encode()), seed]).standard_normal(out[name].shape)
        drawn = base * np.exp(spread * noise) if base else spread * noise
        out[name] = jnp.asarray(drawn.astype(out[name].dtype))
    for name, factor in factors.items():
        out[name] = (out[name] * factor).astype(out[name].dtype)
    return out
```

```python
from contextlib import ExitStack

import concourse.bass as bass
from concourse import mybir

F32 = mybir.dt.float32
F16 = mybir.dt.float16
ALU = mybir.AluOpType
ACT = mybir.ActivationFunctionType
AX = mybir.AxisListType

B, N, K, D, H = 8, 256, 256, 256, 1024
ROUNDS = 3
P = 128
C2 = D // P
J2 = N // P
HT = H // P
HALF = 512
LOGIT_SCALE = float(D) ** 0.5
EPS_ATTN = 1e-8
LN_EPS = 1e-5
EPS_TERNARY = 1e-6
RING = 2

COL = {name: C2 * i for i, name in enumerate(
    ["lnkv_g", "lnkv_b", "lnq_g", "lnm_g", "lnm_b", "bk", "bv", "b1"])}
COL_LNB = C2 * len(COL)
NCOL = COL_LNB + HT
ROW = {name: D * i for i, name in enumerate(
    ["q_mu", "q_logsig", "lnq_g", "lnp_g", "lnp_b", "b2", "bu"])}
ROW_LNW = D * len(ROW)
ROW_COND = ROW_LNW + H
NROW = ROW_COND + B * D


def build(nc, x, ctx_in, w_nat, w_tr, w_fc_t, w_proj_t, cols, rows, out):
    with ExitStack() as stack:
        def sb(name, shape, dt=F32):
            return stack.enter_context(nc.sbuf_tensor(name, [P] + shape, dt))

        def sem(name):
            return stack.enter_context(nc.semaphore(name))

        ps_t = [stack.enter_context(nc.psum_tensor(f"ps_t{i}", [P, HALF], F32)) for i in range(2)]
        ps_mid = [stack.enter_context(nc.psum_tensor(f"ps_mid{i}", [P, HALF], F32)) for i in range(2)]
        ps_low = [stack.enter_context(nc.psum_tensor(f"ps_low{i}", [P, 2, HALF], F32)) for i in range(2)]

        X = sb("X", [B, J2, D])
        S = sb("S", [B, J2, D])
        Y = sb("Y", [B, J2, D])
        XH = sb("XH", [B, J2, D])
        KT = sb("KT", [B, C2, N])
        V = sb("V", [B, J2, D + 2])
        XT = sb("XT", [2, C2, K])
        PR = sb("PR", [4, J2, K])
        GT = sb("GT", [4, C2, K])
        wn = sb("wn", [5, C2, D])
        wt = sb("wt", [3, C2, D])
        Wkq = sb("Wkq", [C2, D])
        Wvu = sb("Wvu", [C2, D])
        wf = sb("wf", [2 * H // P * D])
        WfT = sb("WfT", [C2, H], F16)
        WpT = sb("WpT", [HT, D], F16)
        colv = sb("colv", [NCOL])
        rowv = sb("rowv", [NROW])
        vbias = sb("vbias", [J2, D])
        lnb_out = sb("lnb_out", [J2, D])
        gain2 = sb("gain2", [J2, D])
        shift2 = sb("shift2", [J2, D])
        ident = sb("ident", [P])
        ones = sb("ones", [P])
        bcol = sb("bcol", [HT, P])
        ckv = sb("ckv", [4, 1])
        kbias = sb("kbias", [C2])
        b1fold = sb("b1fold", [C2])
        absum = sb("absum", [2])
        thr = sb("thr", [2, 2])
        nmax = sb("nmax", [B, J2])
        rsum = sb("rsum", [B, J2])
        rinv = sb("rinv", [B, J2])
        cinv = sb("cinv", [B, J2, 1])
        mhalf = sb("mhalf", [J2])

        cond_row = rowv[:, ROW_COND:].rearrange("p (b d) -> p b d", b=B)

        def row(name):
            return rowv[:, ROW[name]:ROW[name] + D]

        def col(name, c):
            return colv[:, COL[name] + c:COL[name] + c + 1]

        WK, WV, WU, W1, W2 = range(5)
        TK, TQ, TV = range(3)
        W1g = wt[:, TK]
        wfc_raw = wf[:, 0:C2 * H].rearrange("p (c h) -> p c h", c=C2)
        wproj_raw = wf[:, C2 * H:].rearrange("p (h d) -> p h d", h=HT)
        Gf = KT[:, :, :, :].rearrange("p b c n -> p (b c n)")[:, 0:2 * H].rearrange("p (r h) -> p r h", r=2)
        GC = KT[:, :, :, :].rearrange("p b c n -> p (b c n)")[:, 2 * H:4 * H].rearrange("p (r h) -> p r h", r=2)
        XR = PR[:, 0:2]
        vf = V[:, :, :, :].rearrange("p b j d -> p (b j d)")

        def halves(at, n):
            return vf[:, at:at + n // 2].bitcast(F16)

        XTh = halves(0, 2 * C2 * N).rearrange("p (u c k) -> p u c k", u=2, c=C2)
        XTl = halves(C2 * N, 2 * C2 * N).rearrange("p (u c k) -> p u c k", u=2, c=C2)
        GTh = halves(2 * C2 * N, 2 * HT * P).rearrange("p (r t k) -> p r t k", r=2, t=HT)
        GTl = halves(2 * C2 * N + HT * P, 2 * HT * P).rearrange("p (r t k) -> p r t k", r=2, t=HT)

        class Norm:

            def __init__(self, name, slots=B, tiles=J2, applied=None):
                self.tiles = tiles
                self.slots = slots
                self.applied = applied
                self.st = sb(f"{name}_st", [slots, tiles, 2, 6])
                self.mv = sb(f"{name}_mv", [slots, tiles, 2])
                self.ve = sb(f"{name}_ve", [slots, tiles])
                self.nm = sb(f"{name}_nm", [slots, tiles])
                self.ab = sb(f"{name}_ab", [slots, 2, tiles])
                self.stats_done = sem(f"{name}_stats_done")
                self.moments = sem(f"{name}_moments")
                self.chain = sem(f"{name}_chain")
                self.coef = sem(f"{name}_coef")


        ctx_in_sem = [sem(f"ctx_in{b}") for b in range(B)]
        x_in_sem = [sem(f"x_in{b}") for b in range(B)]
        vec_in = sem("vec_in")
        wkq_in = sem("wkq_in")
        wvu_in = sem("wvu_in")
        mlp_in = sem("mlp_in")
        ffn_in = sem("ffn_in")
        stored = sem("stored")
        consts = sem("consts")
        w_prod = sem("w_prod")
        w_fold = sem("w_fold")
        sig_ready = sem("sig_ready")
        spread = sem("spread")
        ymul = sem("ymul")
        xc_ready = sem("xc_ready")
        xx_ready = sem("xx_ready")
        xq_ready = sem("xq_ready")
        xm_ready = sem("xm_ready")
        xp_ready = sem("xp_ready")
        xf_ready = sem("xf_ready")
        y_ready = sem("y_ready")
        s_shifted = sem("s_shifted")
        t_ready = sem("t_ready")
        t_copied = sem("t_copied")
        mid_ready = sem("mid_ready")
        mid_read = sem("mid_read")
        low_ready = sem("low_ready")
        low_read = sem("low_read")
        kv_stored = sem("kv_stored")
        max_ready = sem("max_ready")
        rinv_ready = sem("rinv_ready")
        attn_ready = sem("attn_ready")
        cinv_ready = sem("cinv_ready")
        tern_fold = sem("tern_fold")
        tern_sum = sem("tern_sum")
        tern_cast = sem("tern_cast")
        x1_ready = sem("x1_ready")
        x1_shifted = sem("x1_shifted")
        xth_ready = sem("xth_ready")
        xtl_ready = sem("xtl_ready")
        f1_ready = sem("f1_ready")
        gelu_done = sem("gelu_done")
        gc_done = sem("gc_done")
        tg_ready = sem("tg_ready")
        gth_ready = sem("gth_ready")
        gtl_ready = sem("gtl_ready")
        o_ready = sem("o_ready")
        o_done = sem("o_done")

        lnc, lnx, lnf = Norm("lnc", 2, J2, xc_ready), Norm("lnx", 2, J2, xx_ready), Norm("lnf", 2, J2, xf_ready)
        lnq, lnm, lnp = Norm("lnq"), Norm("lnm"), Norm("lnp")
        lng = Norm("lng", 2, 1, o_done)

        x_v = x.rearrange("b (p j) d -> b p (j d)", j=J2)
        c_v = ctx_in.rearrange("b (p j) d -> b p (j d)", j=J2)
        o_v = out.rearrange("b (p j) d -> b p (j d)", j=J2)

        dve_held, pool_held = sem("dve_held"), sem("pool_held")

        def flat(t, b):
            return t[:, b].rearrange("p j d -> p (j d)")

        def pairs(eng, step, lo=1, hi=B // 2 - 1):
            for b in range(2 * lo):
                step(b, b % 2, b, None)
            with eng.Fori(lo, hi) as i:
                for u in range(2):
                    step(2 * i + u, u, None, None)
            for b in range(2 * hi, B):
                step(b, b % 2, None, b)

        def ln_stats(dve, ln, n, at, tiles):
            parts = 2 if tiles[0].shape[-1] > HALF else 1
            for j, tile in enumerate(tiles):
                w = tile.shape[-1] // parts
                for h in range(parts):
                    last = dve.bn_stats(ln.st[:, at, j, h], tile[:, h * w:(h + 1) * w])
                    last.then_inc(ln.stats_done, 1)
            ln_moments(dve, ln, n, at, parts)

        def ln_moments(dve, ln, n, at, parts):
            if ln.slots == 2 and not (isinstance(n, int) and n < 2):
                dve.wait_ge(ln.coef, n - 1)
            dve.wait_ge(ln.stats_done, (n + 1) * (ln.tiles * parts))
            dve.sem_inc(dve_held, 1)
            for j in range(ln.tiles):
                dve.bn_aggr(ln.mv[:, at, j], ln.st[:, at, j, 0:parts].rearrange("p h s -> p (h s)"))\
                   .then_inc(ln.moments, 1)

        def ln_coef(pool, ln, n, at):
            if ln.slots == 2 and not (isinstance(n, int) and n < 2):
                pool.wait_ge(ln.applied, n - 1)
            pool.wait_ge(ln.moments, (n + 1) * ln.tiles)
            pool.sem_inc(pool_held, 1)
            pool.tensor_scalar(ln.ve[:, at], ln.mv[:, at, :, 1], LN_EPS, None, ALU.add).then_inc(ln.chain, 1)
            pool.tensor_scalar(ln.nm[:, at], ln.mv[:, at, :, 0], -1.0, None, ALU.mult).then_inc(ln.chain, 1)
            pool.wait_ge(ln.chain, n * 3 + 2)
            pool.tensor_tensor(ln.ab[:, at, 0], ln.ve[:, at], mhalf[:, 0:ln.tiles], ALU.pow).then_inc(ln.chain, 1)
            pool.wait_ge(ln.chain, n * 3 + 3)
            pool.tensor_tensor(ln.ab[:, at, 1], ln.nm[:, at], ln.ab[:, at, 0], ALU.mult).then_inc(ln.coef, 1)

        def ln_apply(act, ln, n, at, src, dst, ready):
            act.wait_ge(ln.coef, n + 1)
            for j in range(J2):
                last = act.activation(dst[:, j], src[:, j], ACT.Identity,
                                      bias=ln.ab[:, at, 1, j:j + 1], scale=ln.ab[:, at, 0, j:j + 1])
            last.then_inc(ready, 1)

        def transposes(pe, s, u, src):
            pe.wait_ge(t_copied, s + 1)
            for c in range(C2):
                for j in range(J2):
                    last = pe.transpose(ps_t[u][:, c * K + j * P:c * K + (j + 1) * P],
                                        src[:, j, c * P:(c + 1) * P], ident[:])
            last.then_inc(t_ready, 1)

        def copy_xt(act, s, u):
            act.wait_ge(t_ready, s + 1)
            act.wait_ge(mid_ready, s + 1)
            act.activation(XT[:, u].rearrange("p c k -> p (c k)"), ps_t[u][:], ACT.Copy).then_inc(t_copied, 1)

        block = stack.enter_context(nc.Block())

        def ring(t, b, second):
            return t * (2 * B) + (B + b + (B if second else 0))

        T_FFN = B + ROUNDS * 2 * B

        FOLD_CK, FOLD_CV, FOLD_KQ, FOLD_KB, FOLD_VU, FOLD_VB, FOLD_W1 = 1, 2, 4, 6, 8, 10, 17
        TERN_MADE, TERN_DONE = 8, 18

        @block.sync
        def _(sp):
            def load(dst, src, s):
                sp.dma_start(dst, src).then_inc(s, 16)

            load(S[:, 0].rearrange("p j d -> p (j d)"), c_v[0], ctx_in_sem[0])
            load(wn[:, WK].rearrange("p c d -> p (c d)"), w_nat[0], wkq_in)
            load(wt[:, TK:TQ + 1].rearrange("p w c d -> p w (c d)"), w_tr[0:2].rearrange("w p n -> p w n"), wkq_in)
            load(colv[:], cols, vec_in)
            load(rowv[:], rows.rearrange("(a n) -> a n", a=1).broadcast_to([P, NROW]), vec_in)
            load(wn[:, WV:WU + 1].rearrange("p w c d -> p w (c d)"), w_nat[1:3].rearrange("w p n -> p w n"), wvu_in)
            load(wt[:, TV].rearrange("p c d -> p (c d)"), w_tr[2], wvu_in)
            for b in range(B):
                if b:
                    load(flat(S, b), c_v[b], ctx_in_sem[b])
                load(flat(X, b), x_v[b], x_in_sem[b])
            load(wn[:, W1:W2 + 1].rearrange("p w c d -> p w (c d)"), w_nat[3:5].rearrange("w p n -> p w n"), mlp_in)
            load(wf[:, 0:C2 * H], w_fc_t, ffn_in)
            load(wf[:, C2 * H:], w_proj_t, ffn_in)
            with sp.Fori(0, B) as b:
                sp.wait_ge(o_done, 2 * b + 2)
                sp.dma_start(o_v[b], flat(X, b)).then_inc(stored, 16)
            sp.wait_ge(stored, 16 * B)

        @block.gpsimd
        def _(pool):
            pool.memset(ident[:], 0.0).then_inc(consts, 1)
            pool.memset(ones[:], 1.0).then_inc(consts, 1)
            pool.memset(mhalf[:], -0.5).then_inc(consts, 1)
            pool.memset(V[:, :, :, D:D + 1], 1.0).then_inc(consts, 1)
            pool.wait_ge(consts, 1)
            pool.affine_select(out=ident[:], in_=ident[:], compare_op=ALU.not_equal, fill=1.0, base=0,
                               pattern=[[-1, P]], channel_multiplier=1).then_inc(consts, 1)
            pool.wait_ge(consts, 5)

            pool.wait_ge(vec_in, 32)
            for b in range(B):
                pool.tensor_tensor(cond_row[:, b], cond_row[:, b], row("b2"), ALU.add).then_inc(consts, 1)

            def init_y(b, u):
                pool.wait_ge(ymul, b + 1)
                pool.sem_inc(pool_held, 1)
                for j in range(J2):
                    pool.tensor_tensor(Y[:, b, j], XH[:, b, j], row("q_mu"), ALU.add).then_inc(y_ready, 1)

            def prologue(b, u, first, last):
                if last is None or last < B - 1:
                    ln_coef(pool, lnc, b + 1, 1 - u)
                ln_coef(pool, lnx, b, u)
                if first is None or first >= 1:
                    init_y(b - 1, 1 - u)

            ln_coef(pool, lnc, 0, 0)
            pairs(pool, prologue)
            init_y(B - 1, 1)

            pool.wait_ge(consts, 5 + B)
            with pool.Fori(0, ROUNDS) as t:
                def shift_s(b):
                    pool.wait_ge(xm_ready, t * B + (b + 1))
                    for j in range(J2):
                        pool.tensor_tensor(S[:, b, j], S[:, b, j], cond_row[:, b], ALU.add).then_inc(s_shifted, 1)

                for b in range(2):
                    ln_coef(pool, lnq, t * B + b, b)
                for j in range(B + 4):
                    if j + 2 < B:
                        ln_coef(pool, lnq, t * B + (j + 2), j + 2)
                    if 0 <= j - 3 < B:
                        ln_coef(pool, lnm, t * B + (j - 3), j - 3)
                    if 0 <= j - 4 < B:
                        shift_s(j - 4)
                for j in range(3, B + 4):
                    if j - 3 < B:
                        ln_coef(pool, lnp, t * B + (j - 3), j - 3)
                    if 0 <= j - 4 < B:
                        b = j - 4
                        pool.wait_ge(ymul, t * B + (B + b + 1))
                        pool.tensor_tensor(flat(Y, b), flat(XH, b), shift2[:].rearrange("p j d -> p (j d)"),
                                           ALU.add).then_inc(y_ready, 2)

            def ffn_x1(b, u):
                pool.wait_ge(y_ready, 2 * (ROUNDS + 1) * B)
                pool.tensor_tensor(flat(X, b), flat(X, b), flat(Y, b), ALU.add).then_inc(x1_ready, 1)

            def ffn_shift(b):
                pool.wait_ge(xf_ready, b + 1)
                pool.wait_ge(x1_ready, b + 1)
                pool.sem_inc(pool_held, 1)
                pool.tensor_tensor(flat(X, b), flat(X, b), lnb_out[:].rearrange("p j d -> p (j d)"),
                                   ALU.add).then_inc(x1_shifted, 1)

            pool.wait_ge(tern_fold, TERN_DONE)
            ffn_x1(0, 0)
            ln_coef(pool, lnf, 0, 0)

            def ffn(b, u, first, last):
                if last is None or last < B - 1:
                    ffn_x1(b + 1, 1 - u)
                    ln_coef(pool, lnf, b + 1, 1 - u)
                ffn_shift(b)
                for rt in range(2):
                    ln_coef(pool, lng, 2 * b + rt, rt)

            pairs(pool, ffn)

        @block.scalar
        def _(act):
            act.sem_inc(t_copied, RING)
            act.sem_inc(mid_read, 2 * RING)
            act.wait_ge(vec_in, 32)
            act.activation(row("q_logsig"), row("q_logsig"), ACT.Exp).then_inc(sig_ready, 1)

            ln_apply(act, lnc, 0, 0, S[:, 0], XR[:, 0], xc_ready)

            def prologue(b, u, first, last):
                copy_xt(act, b, u)
                if last is None or last < B - 1:
                    ln_apply(act, lnc, b + 1, 1 - u, S[:, b + 1], XR[:, 1 - u], xc_ready)
                act.wait_ge(w_fold, FOLD_KB)
                act.wait_ge(mid_ready, b + (1 + RING))
                for c in range(C2):
                    act.activation(KT[:, b, c], ps_mid[u][:, c * N:(c + 1) * N], ACT.Identity,
                                   bias=kbias[:, c:c + 1], scale=LOGIT_SCALE).then_inc(mid_read, 1)
                ln_apply(act, lnx, b, u, X[:, b], XH[:, b], xx_ready)

            pairs(act, prologue)

            with act.Fori(0, ROUNDS) as t:
                def exps(b):
                    s = ring(t, b, False)
                    act.wait_ge(max_ready, t * B + (b + 1))
                    if b >= 4:
                        act.wait_ge(low_ready, s - 4 + 1)
                    for j in range(J2):
                        act.activation(PR[:, b % 4, j], ps_mid[b % 2][:, j * K:(j + 1) * K], ACT.Exp,
                                       bias=nmax[:, b, j:j + 1], accum_out=rsum[:, b, j:j + 1])\
                           .then_inc(mid_read, 1)

                def gelus(b):
                    s = ring(t, b, True)
                    act.wait_ge(mid_ready, s + (1 + RING))
                    if b >= 4:
                        act.wait_ge(low_ready, s - 4 + 1)
                    for c in range(C2):
                        act.activation(GT[:, b % 4, c], ps_mid[b % 2][:, c * K:(c + 1) * K], ACT.Gelu,
                                       bias=b1fold[:, c:c + 1]).then_inc(mid_read, 1)

                ln_apply(act, lnq, t * B, 0, Y[:, 0], XH[:, 0], xq_ready)
                for j in range(B + 4):
                    if j + 1 < B:
                        ln_apply(act, lnq, t * B + (j + 1), j + 1, Y[:, j + 1], XH[:, j + 1], xq_ready)
                    if j < B:
                        copy_xt(act, ring(t, j, False), j % 2)
                    if 0 <= j - 1 < B:
                        exps(j - 1)
                    if 0 <= j - 4 < B:
                        b = j - 4
                        ln_apply(act, lnm, t * B + b, b, S[:, b], XH[:, b], xm_ready)
                for j in range(B + 4):
                    if j < B:
                        copy_xt(act, ring(t, j, True), j % 2)
                    if 0 <= j - 1 < B:
                        gelus(j - 1)
                    if 0 <= j - 4 < B:
                        b = j - 4
                        ln_apply(act, lnp, t * B + b, b, S[:, b], XH[:, b], xp_ready)

            act.wait_ge(tern_fold, TERN_MADE)
            act.activation(WfT[:].rearrange("p c h -> p (c h)"), wf[:, 0:C2 * H], ACT.Copy).then_inc(tern_cast, 1)
            act.activation(WpT[:].rearrange("p t d -> p (t d)"), wf[:, C2 * H:], ACT.Copy).then_inc(tern_cast, 1)

            def copy_high(b, u):
                act.wait_ge(t_ready, b + (T_FFN + 1))
                if not (isinstance(b, int) and b < 2):
                    act.wait_ge(f1_ready, 4 * b - 4)
                act.activation(XTh[:, u].rearrange("p c k -> p (c k)"), ps_t[0][:], ACT.Copy).then_inc(xth_ready, 1)

            def gelu_half(r, rt, h):
                act.wait_ge(f1_ready, 2 * r + (h + 1))
                if not (isinstance(r, int) and r < 2):
                    act.wait_ge(gc_done, 2 * r - 2)
                act.activation(Gf[:, rt, h * HALF:(h + 1) * HALF], ps_mid[h][:], ACT.Gelu).then_inc(gelu_done, 1)

            def high_half(r, rt, h):
                act.wait_ge(tg_ready, 2 * r + (h + 1))
                if not (isinstance(r, int) and r < 2):
                    act.wait_ge(o_ready, r - 1)
                act.activation(GTh[:, rt, 4 * h:4 * h + 4].rearrange("p t k -> p (t k)"), ps_low[rt][:, h],
                               ACT.Copy).then_inc(gth_ready, 1)

            ln_apply(act, lnf, 0, 0, X[:, 0], XR[:, 0], xf_ready)
            copy_high(0, 0)

            def ffn(b, u, first, last):
                for rt in range(2):
                    r = 2 * b + rt
                    gelu_half(r, rt, 0)
                    gelu_half(r, rt, 1)
                    if rt == 0 and (last is None or last < B - 1):
                        ln_apply(act, lnf, b + 1, 1 - u, X[:, b + 1], XR[:, 1 - u], xf_ready)
                    if rt == 1 or first != 0:
                        high_half(r - 1, 1 - rt, 0)
                        high_half(r - 1, 1 - rt, 1)
                    if rt == 0 and (last is None or last < B - 1):
                        copy_high(b + 1, 1 - u)

            pairs(act, ffn)
            for h in range(2):
                high_half(2 * B - 1, 1, h)

        @block.vector
        def _(dve):
            dve.sem_inc(low_read, 2 * RING)
            dve.wait_ge(ctx_in_sem[0], 16)
            ln_stats(dve, lnc, 0, 0, [S[:, 0, j] for j in range(J2)])

            dve.wait_ge(w_prod, 1)
            dve.tensor_tensor(ckv[:, 0:2, 0], ps_low[0][:, 0, 0:2], colv[:, COL["bk"]:COL["bk"] + 2],
                              ALU.add).then_inc(w_fold, 1)
            dve.wait_ge(w_prod, 2)
            dve.tensor_tensor(ckv[:, 2:4, 0], ps_low[0][:, 1, 0:2], colv[:, COL["bv"]:COL["bv"] + 2],
                              ALU.add).then_inc(w_fold, 1)
            dve.wait_ge(w_prod, 3)
            for c in range(C2):
                dve.scalar_tensor_tensor(out=Wkq[:, c], in0=ps_mid[0][:, c * D:(c + 1) * D], scalar=col("lnkv_g", c),
                                         in1=row("lnq_g"), op0=ALU.mult, op1=ALU.mult).then_inc(w_fold, 1)
            dve.wait_ge(w_prod, 4)
            for c in range(C2):
                dve.tensor_scalar(kbias[:, c:c + 1], ps_low[1][:, 0, c:c + 1], col("lnq_g", c), LOGIT_SCALE,
                                  ALU.mult, ALU.mult).then_inc(w_fold, 1)
            dve.wait_ge(w_prod, 5)
            for c in range(C2):
                dve.tensor_scalar(Wvu[:, c], ps_mid[1][:, c * D:(c + 1) * D], col("lnkv_g", c), None,
                                  ALU.mult).then_inc(w_fold, 1)
            dve.wait_ge(w_fold, FOLD_CV)
            dve.wait_ge(consts, 5)
            for c in range(C2):
                dve.tensor_scalar(bcol[:, c], ones[:], ckv[:, 2 + c], None, ALU.mult).then_inc(spread, 1)
            dve.wait_ge(w_prod, 6)
            for j in range(J2):
                dve.tensor_tensor(vbias[:, j], ps_low[1][:, 1, 0:D], row("bu"), ALU.add).then_inc(w_fold, 1)

            def stats_c(b, u):
                ln_stats(dve, lnc, b, u, [S[:, b, j] for j in range(J2)])

            def stats_x(b, u):
                ln_stats(dve, lnx, b, u, [X[:, b, j] for j in range(J2)])

            def v_copy(b, u):
                dve.wait_ge(low_ready, b + 1)
                dve.tensor_tensor(V[:, b, :, 0:D], ps_low[u][:, 0].rearrange("p (j d) -> p j d", j=J2), vbias[:],
                                  ALU.add).then_inc(low_read, 2)

            def mul_sig(b):
                dve.wait_ge(xx_ready, b + 1)
                if isinstance(b, int) and b == 0:
                    dve.wait_ge(sig_ready, 1)
                for j in range(J2):
                    last = dve.tensor_tensor(XH[:, b, j], XH[:, b, j], row("q_logsig"), ALU.mult)
                last.then_inc(ymul, 1)

            for b in range(1, B):
                dve.wait_ge(ctx_in_sem[b], 16)
                dve.wait_ge(x_in_sem[b - 1], 16)
                if b == 1:
                    stats_c(1, 1)
                if b == B - 1:
                    dve.wait_ge(x_in_sem[B - 1], 16)

            def prologue(b, u, first, last):
                if last is None:
                    stats_c(b + 2, u)
                v_copy(b, u)
                stats_x(b, u)
                if first is None or first >= 1:
                    mul_sig(b - 1)

            pairs(dve, prologue)
            mul_sig(B - 1)

            dve.wait_ge(mlp_in, 16)
            for c in range(C2):
                dve.tensor_scalar(W1g[:, c], wn[:, W1, c], col("lnm_g", c), None, ALU.mult).then_inc(w_fold, 1)
            for j in range(J2):
                dve.tensor_copy(gain2[:, j], row("lnp_g")).then_inc(w_fold, 1)
                dve.tensor_copy(shift2[:, j], row("lnp_b")).then_inc(w_fold, 1)
            dve.wait_ge(w_prod, 7)
            dve.tensor_tensor(b1fold[:], ps_low[0][:, 0, 0:2], colv[:, COL["b1"]:COL["b1"] + 2],
                              ALU.add).then_inc(w_fold, 1)
            dve.wait_ge(ffn_in, 32)
            for i, raw in enumerate((wf[:, 0:C2 * H], wf[:, C2 * H:])):
                dve.tensor_reduce(absum[:, i:i + 1], raw, AX.X, ALU.add, apply_absolute_value=True)\
                   .then_inc(tern_fold, 1)
            dve.wait_ge(tern_sum, 1)
            dve.tensor_scalar(thr[:, 0], ps_low[0][:, 1, 0:2], 1.0 / (H * D), EPS_TERNARY, ALU.mult, ALU.add)\
               .then_inc(tern_fold, 1)
            dve.wait_ge(tern_fold, 3)
            dve.tensor_scalar(thr[:, 1], thr[:, 0], -0.5, None, ALU.mult).then_inc(tern_fold, 1)
            dve.wait_ge(tern_fold, 4)
            dve.tensor_scalar(thr[:, 0], thr[:, 1], -1.0, None, ALU.mult).then_inc(tern_fold, 1)
            dve.wait_ge(tern_fold, 5)
            below = S[:, 0:4].rearrange("p b j d -> p (b j d)")
            for i, raw in enumerate((wf[:, 0:C2 * H], wf[:, C2 * H:])):
                dve.tensor_scalar(below, raw, thr[:, 1, i:i + 1], None, ALU.is_lt).then_inc(spread, 1)
                dve.wait_ge(spread, 3 + i)
                dve.scalar_tensor_tensor(out=raw, in0=raw, scalar=thr[:, 0, i:i + 1], in1=below,
                                         op0=ALU.is_gt, op1=ALU.subtract).then_inc(tern_fold, 1)
                dve.wait_ge(tern_fold, 6 + i)
            for k in range(HT):
                last = dve.tensor_scalar(bcol[:, k], ones[:], colv[:, COL_LNB + k:COL_LNB + k + 1], None, ALU.mult)
            last.then_inc(tern_fold, 1)
            dve.wait_ge(tern_sum, 2)
            for j in range(J2):
                dve.tensor_copy(lnb_out[:, j], ps_low[1][:, 0, 0:D]).then_inc(tern_fold, 5)

            dve.wait_ge(w_fold, FOLD_W1)
            with dve.Fori(0, ROUNDS) as t:
                def stats_q(b):
                    dve.wait_ge(y_ready, t * (2 * B) + (2 * b + 2))
                    ln_stats(dve, lnq, t * B + b, b, [Y[:, b, j] for j in range(J2)])

                def row_max(b):
                    dve.wait_ge(mid_ready, ring(t, b, False) + (1 + RING))
                    dve.tensor_reduce(nmax[:, b], ps_mid[b % 2][:].rearrange("p (j k) -> p j k", j=J2), AX.X,
                                      ALU.max, negate=True).then_inc(max_ready, 1)

                def attention(b):
                    dve.wait_ge(mid_read, ring(t, b, False) * 2 + (2 + 2 * RING))
                    dve.reciprocal(rinv[:, b], rsum[:, b]).then_inc(rinv_ready, 1)
                    dve.wait_ge(rinv_ready, t * B + (b + 1))
                    for j in range(J2):
                        dve.tensor_scalar(PR[:, b % 4, j], PR[:, b % 4, j], rinv[:, b, j:j + 1], EPS_ATTN,
                                          ALU.mult, ALU.add).then_inc(attn_ready, 1)

                def slots(b):
                    s = ring(t, b, False)
                    dve.wait_ge(low_ready, s + 1)
                    dve.reciprocal(cinv[:, b], ps_low[b % 2][:, :, D:D + 1]).then_inc(cinv_ready, 1)
                    dve.wait_ge(cinv_ready, t * B + (b + 1))
                    for j in range(J2):
                        dve.scalar_tensor_tensor(out=S[:, b, j], in0=ps_low[b % 2][:, j, 0:D], scalar=cinv[:, b, j],
                                                 in1=Y[:, b, j], op0=ALU.mult, op1=ALU.add).then_inc(low_read, 1)
                    dve.wait_ge(low_read, s * 2 + (2 + 2 * RING))
                    ln_stats(dve, lnm, t * B + b, b, [S[:, b, j] for j in range(J2)])

                def slots2(b):
                    s = ring(t, b, True)
                    dve.wait_ge(low_ready, s + 1)
                    dve.wait_ge(s_shifted, t * (2 * B) + (2 * b + 2))
                    dve.tensor_tensor(flat(S, b), ps_low[b % 2][:, 0], flat(S, b), ALU.add).then_inc(low_read, 2)
                    dve.wait_ge(low_read, s * 2 + (2 + 2 * RING))
                    ln_stats(dve, lnp, t * B + b, b, [S[:, b, j] for j in range(J2)])

                def gain(b):
                    dve.wait_ge(xp_ready, t * B + (b + 1))
                    dve.tensor_tensor(flat(XH, b), flat(XH, b), gain2[:].rearrange("p j d -> p (j d)"), ALU.mult)\
                       .then_inc(ymul, 1)

                stats_q(0)
                stats_q(1)
                for j in range(B + 3):
                    if j + 2 < B:
                        stats_q(j + 2)
                    if 0 <= j - 1 < B:
                        row_max(j - 1)
                    if 0 <= j - 2 < B:
                        attention(j - 2)
                    if 0 <= j - 3 < B:
                        slots(j - 3)
                for j in range(3, B + 4):
                    if 0 <= j - 3 < B:
                        slots2(j - 3)
                    if 0 <= j - 4 < B:
                        gain(j - 4)

            def stats_f(b, u):
                dve.wait_ge(x1_ready, b + 1)
                ln_stats(dve, lnf, b, u, [X[:, b, j] for j in range(J2)])

            def low_parts(b, u):
                dve.wait_ge(xth_ready, b + 1)
                if not (isinstance(b, int) and b < 2):
                    dve.wait_ge(f1_ready, 4 * b - 4)
                dve.tensor_tensor(XTl[:, u].rearrange("p c k -> p (c k)"), ps_t[0][:],
                                  XTh[:, u].rearrange("p c k -> p (c k)"), ALU.subtract).then_inc(xtl_ready, 1)

            def centre(r, rt):
                for h in range(2):
                    dve.wait_ge(gelu_done, 2 * r + (h + 1))
                    dve.bn_stats(lng.st[:, rt, 0, h], Gf[:, rt, h * HALF:(h + 1) * HALF]).then_inc(lng.stats_done, 1)
                if not (isinstance(r, int) and r < 2):
                    dve.wait_ge(tg_ready, 2 * r - 2)
                ln_moments(dve, lng, r, rt, 2)
                dve.wait_ge(lng.moments, r + 1)
                for h in range(2):
                    dve.scalar_tensor_tensor(out=GC[:, rt, h * HALF:(h + 1) * HALF],
                                             in0=Gf[:, rt, h * HALF:(h + 1) * HALF], scalar=lng.mv[:, rt, 0, 0:1],
                                             in1=rowv[:, ROW_LNW + h * HALF:ROW_LNW + (h + 1) * HALF],
                                             op0=ALU.subtract, op1=ALU.mult).then_inc(gc_done, 1)

            def low_half(r, rt, h):
                dve.wait_ge(gth_ready, 2 * r + (h + 1))
                if not (isinstance(r, int) and r < 2):
                    dve.wait_ge(o_ready, r - 1)
                dve.tensor_tensor(GTl[:, rt, 4 * h:4 * h + 4].rearrange("p t k -> p (t k)"), ps_low[rt][:, h],
                                  GTh[:, rt, 4 * h:4 * h + 4].rearrange("p t k -> p (t k)"), ALU.subtract)\
                   .then_inc(gtl_ready, 1)

            def result(b, r, rt):
                dve.wait_ge(o_ready, r + 1)
                dve.wait_ge(lng.coef, r + 1)
                dve.wait_ge(x1_shifted, b + 1)
                dve.scalar_tensor_tensor(out=X[:, b, rt], in0=ps_t[1][:, 0:D], scalar=lng.ab[:, rt, 0, 0:1],
                                         in1=X[:, b, rt], op0=ALU.mult, op1=ALU.add).then_inc(o_done, 1)

            stats_f(0, 0)
            low_parts(0, 0)

            def ffn(b, u, first, last):
                for rt in range(2):
                    r = 2 * b + rt
                    if rt == 0 and (last is None or last < B - 1):
                        stats_f(b + 1, 1 - u)
                    centre(r, rt)
                    if rt == 1 or first != 0:
                        low_half(r - 1, 1 - rt, 0)
                        low_half(r - 1, 1 - rt, 1)
                    if rt == 0 and (last is None or last < B - 1):
                        low_parts(b + 1, 1 - u)
                    if first != 0:
                        result(b - 1, r - 2, rt)

            pairs(dve, ffn)
            result(B - 1, 2 * B - 2, 0)
            for h in range(2):
                low_half(2 * B - 1, 1, h)
            result(B - 1, 2 * B - 1, 1)

        @block.tensor
        def _(pe):
            pe.sem_inc(mid_ready, RING)
            pe.wait_ge(wkq_in, 32)
            pe.wait_ge(vec_in, 32)

            def column(dst, w, v, o):
                for m in range(C2):
                    for c in range(C2):
                        last = pe.matmul(dst[:, m:m + 1], w[:, c, m * P:(m + 1) * P], v(c),
                                         start=(c == 0), stop=(c == C2 - 1))
                return last

            column(ps_low[0][:, 0], wn[:, WK], lambda c: col("lnkv_b", c), 0).then_inc(w_prod, 1)
            pe.wait_ge(wvu_in, 32)
            column(ps_low[0][:, 1], wn[:, WV], lambda c: col("lnkv_b", c), 0).then_inc(w_prod, 1)

            def product(dst, at, bt):
                for m in range(C2):
                    for c in range(C2):
                        last = pe.matmul(dst[:, m * D:(m + 1) * D], at[:, c, m * P:(m + 1) * P], bt[:, c],
                                         start=(c == 0), stop=(c == C2 - 1))
                return last

            product(ps_mid[0], wt[:, TK], wt[:, TQ]).then_inc(w_prod, 1)
            pe.wait_ge(w_fold, FOLD_CK)
            column(ps_low[1][:, 0], wt[:, TQ], lambda c: ckv[:, c], 0).then_inc(w_prod, 1)
            product(ps_mid[1], wt[:, TV], wn[:, WU]).then_inc(w_prod, 1)
            pe.wait_ge(spread, 2)
            for c in range(C2):
                last = pe.matmul(ps_low[1][:, 1, 0:D], bcol[:, c], wn[:, WU, c], start=(c == 0), stop=(c == C2 - 1))
            last.then_inc(w_prod, 1)

            pe.wait_ge(consts, 5)

            def context_t(b, u):
                pe.wait_ge(xc_ready, b + 1)
                transposes(pe, b, u, XR[:, u])

            def keys_values(b, u):
                pe.wait_ge(t_copied, b + (1 + RING))
                if isinstance(b, int) and b == 0:
                    pe.wait_ge(w_fold, FOLD_VB)
                pe.wait_ge(low_read, 2 * b + 2)
                for j in range(J2):
                    for c in range(C2):
                        last = pe.matmul(ps_low[u][:, 0, j * D:(j + 1) * D], XT[:, u, c, j * P:(j + 1) * P], Wvu[:, c],
                                         start=(c == 0), stop=(c == C2 - 1))
                last.then_inc(low_ready, 1)
                pe.wait_ge(mid_read, 2 * b + 2)
                for m in range(C2):
                    for c in range(C2):
                        last = pe.matmul(ps_mid[u][:, m * N:(m + 1) * N], Wkq[:, c, m * P:(m + 1) * P], XT[:, u, c],
                                         start=(c == 0), stop=(c == C2 - 1))
                last.then_inc(mid_ready, 1)

            context_t(0, 0)

            def prologue(b, u, first, last):
                if last is None or last < B - 1:
                    context_t(b + 1, 1 - u)
                keys_values(b, u)

            pairs(pe, prologue)

            pe.wait_ge(mlp_in, 16)
            pe.wait_ge(low_read, 2 * B + 2 * RING)
            column(ps_low[0][:, 0], wn[:, W1], lambda c: col("lnm_b", c), 0).then_inc(w_prod, 1)
            pe.wait_ge(tern_fold, 2)
            pe.matmul(ps_low[0][:, 1, 0:2], ones[:], absum[:], start=True, stop=True).then_inc(tern_sum, 1)
            pe.wait_ge(tern_fold, TERN_MADE)
            for k in range(HT):
                last = pe.matmul(ps_low[1][:, 0, 0:D], bcol[:, k], wproj_raw[:, k], start=(k == 0), stop=(k == HT - 1))
            last.then_inc(tern_sum, 1)
            pe.wait_ge(tern_fold, TERN_DONE)
            pe.wait_ge(w_fold, FOLD_W1)

            with pe.Fori(0, ROUNDS) as t:
                def logits(b):
                    s = ring(t, b, False)
                    pe.wait_ge(t_copied, s + (1 + RING))
                    pe.wait_ge(mid_read, s * 2 + 2)
                    u = b % 2
                    for j in range(J2):
                        for c in range(C2):
                            last = pe.matmul(ps_mid[u][:, j * K:(j + 1) * K], KT[:, b, c, j * P:(j + 1) * P],
                                             XT[:, u, c], start=(c == 0), stop=(c == C2 - 1))
                    last.then_inc(mid_ready, 1)

                def update(b):
                    s = ring(t, b, False)
                    pe.wait_ge(attn_ready, t * (2 * B) + (2 * b + 2))
                    pe.wait_ge(low_read, s * 2 + 2)
                    for m in range(J2):
                        for j in range(J2):
                            last = pe.matmul(ps_low[b % 2][:, m, 0:D + 1], PR[:, b % 4, j, m * P:(m + 1) * P],
                                             V[:, b, j, 0:D + 1], start=(j == 0), stop=(j == J2 - 1))
                    last.then_inc(low_ready, 1)

                def hidden(b):
                    s = ring(t, b, True)
                    pe.wait_ge(t_copied, s + (1 + RING))
                    pe.wait_ge(mid_read, s * 2 + 2)
                    u = b % 2
                    for m in range(C2):
                        for c in range(C2):
                            last = pe.matmul(ps_mid[u][:, m * K:(m + 1) * K], W1g[:, c, m * P:(m + 1) * P],
                                             XT[:, u, c], start=(c == 0), stop=(c == C2 - 1))
                    last.then_inc(mid_ready, 1)

                def project(b):
                    s = ring(t, b, True)
                    pe.wait_ge(mid_read, s * 2 + (2 + 2 * RING))
                    pe.wait_ge(low_read, s * 2 + 2)
                    for j in range(J2):
                        for c in range(C2):
                            last = pe.matmul(ps_low[b % 2][:, 0, j * D:(j + 1) * D], GT[:, b % 4, c, j * P:(j + 1) * P],
                                             wn[:, W2, c], start=(c == 0), stop=(c == C2 - 1))
                    last.then_inc(low_ready, 1)

                for second, ready, first_product, second_product in (
                        (False, xq_ready, logits, update), (True, xm_ready, hidden, project)):
                    for j in range(B + 3):
                        if j < B:
                            pe.wait_ge(ready, t * B + (j + 1))
                            transposes(pe, ring(t, j, second), j % 2, XH[:, j])
                        if 0 <= j - 1 < B:
                            first_product(j - 1)
                        if 0 <= j - 3 < B:
                            second_product(j - 3)

            def rows_t(b, u):
                pe.wait_ge(xf_ready, b + 1)
                if isinstance(b, int) and b == 0:
                    pe.wait_ge(t_copied, T_FFN + RING)
                else:
                    pe.wait_ge(xtl_ready, b)
                for c in range(C2):
                    for j in range(J2):
                        last = pe.transpose(ps_t[0][:, c * K + j * P:c * K + (j + 1) * P],
                                            XR[:, u, j, c * P:(c + 1) * P], ident[:])
                last.then_inc(t_ready, 1)

            def fc(b, u, r, rt):
                if rt == 0:
                    pe.wait_ge(xtl_ready, b + 1)
                if isinstance(r, int) and r == 0:
                    pe.wait_ge(tern_cast, 2)
                for h in range(2):
                    if not (isinstance(r, int) and r == 0):
                        pe.wait_ge(gelu_done, 2 * r + (h - 1))
                    k = 0
                    for c in range(C2):
                        for part in (XTh, XTl):
                            last = pe.matmul(ps_mid[h][:], part[:, u, c, rt * P:(rt + 1) * P],
                                             WfT[:, c, h * HALF:(h + 1) * HALF], start=(k == 0), stop=(k == 3))
                            k += 1
                    last.then_inc(f1_ready, 1)

            def hidden_t(r, rt):
                for h in range(2):
                    pe.wait_ge(gc_done, 2 * r + (h + 1))
                    if not (isinstance(r, int) and r < 2):
                        pe.wait_ge(gtl_ready, 2 * r + (h - 3))
                    for k in range(4):
                        last = pe.transpose(ps_low[rt][:, h, k * P:(k + 1) * P],
                                            GC[:, rt, (4 * h + k) * P:(4 * h + k + 1) * P], ident[:])
                    last.then_inc(tg_ready, 1)

            def proj(r, rt):
                pe.wait_ge(gtl_ready, 2 * r + 2)
                if not (isinstance(r, int) and r == 0):
                    pe.wait_ge(o_done, r)
                for k in range(HT):
                    for part in (GTh, GTl):
                        last = pe.matmul(ps_t[1][:, 0:D], part[:, rt, k], WpT[:, k],
                                         start=(k == 0 and part is GTh), stop=(k == HT - 1 and part is GTl))
                last.then_inc(o_ready, 1)

            rows_t(0, 0)

            def ffn(b, u, first, last):
                for rt in range(2):
                    r = 2 * b + rt
                    fc(b, u, r, rt)
                    if rt == 1 or first != 0:
                        hidden_t(r - 1, 1 - rt)
                    if rt == 0 and (last is None or last < B - 1):
                        rows_t(b + 1, 1 - u)
                    if first != 0:
                        proj(r - 2, rt)

            pairs(pe, ffn)
            hidden_t(2 * B - 1, 1)
            proj(2 * B - 2, 0)
            proj(2 * B - 1, 1)


def kernel(**inputs):
    import numpy as np
    import concourse.bacc as bacc
    from concourse.bass_utils import run_bass_kernel_spmd

    g = {k: np.asarray(v) for k, v in inputs.items()}
    xc = {k[len("L0_xcond_"):]: v for k, v in g.items() if k.startswith("L0_xcond_")}

    def tiles(w):
        r, c = w.shape
        return w.reshape(r // P, P, c).transpose(1, 0, 2).reshape(P, -1)

    def columns(v):
        return v.reshape(-1, P).T

    arrays = {
        "x": g["x"],
        "ctx": g["ctx_1024"],
        "w_nat": np.stack([tiles(xc[n]) for n in ("wk", "wv", "wu", "w1", "w2")]),
        "w_tr": np.stack([tiles(xc[n].T) for n in ("wk", "wq", "wv")]),
        "w_fc_t": tiles(g["L0_ffn_W_fc"].T),
        "w_proj_t": tiles(g["L0_ffn_W_proj"].T),
        "cols": np.concatenate([columns(xc[n]) for n in COL] + [columns(g["L0_ffn_ln_b"])], axis=1),
        "rows": np.concatenate([xc[n].reshape(-1) for n in ROW] + [g["L0_ffn_ln_w"], g["cond_1024"].reshape(-1)]),
    }
    arrays = {k: np.ascontiguousarray(v) for k, v in arrays.items()}
    nc = bacc.Bacc("TRN2", target_bir_lowering=False, num_devices=1)
    aps = [nc.dram_tensor(k, v.shape, mybir.dt.from_np(v.dtype), kind="ExternalInput").ap() for k, v in arrays.items()]
    out = nc.dram_tensor("out", g["x"].shape, F32, kind="ExternalOutput").ap()
    build(nc, *aps, out)
    r = run_bass_kernel_spmd(nc, [arrays], core_ids=[0])
    return r.results[0]["out"]
```

```python
from contextlib import ExitStack

import concourse.bass as bass
from concourse import mybir

F32 = mybir.dt.float32
F16 = mybir.dt.float16
ALU = mybir.AluOpType
ACT = mybir.ActivationFunctionType
AX = mybir.AxisListType

B, N, K, D, H = 8, 256, 256, 256, 1024
ROUNDS = 3
P = 128
C2 = D // P
J2 = N // P
HT = H // P
HALF = 512
LOGIT_SCALE = float(D) ** 0.5
EPS_ATTN = 1e-8
LN_EPS = 1e-5
EPS_TERNARY = 1e-6
STEPS = 2 * B
LEAD = 6
CHUNK = 2 * H * D // P // (ROUNDS - 1) // B
RING = 2

COL = {name: C2 * i for i, name in enumerate(
    ["lnkv_g", "lnkv_b", "lnq_g", "lnm_g", "lnm_b", "bk", "bv", "b1"])}
COL_LNB = C2 * len(COL)
NCOL = COL_LNB + HT
ROW = {name: D * i for i, name in enumerate(["bu", "q_mu", "q_logsig", "lnp_g", "lnp_b", "b2"])}
ROWS_EARLY = 3 * D
ROW_LNW = D * len(ROW)
ROW_COND = ROW_LNW + H
NROW = ROW_COND + B * D


def build(nc, x, ctx_in, w_nat, w_tr, w_fc_t, w_proj_t, cols, rows, out):
    with ExitStack() as stack:
        def sb(name, shape, dt=F32):
            return stack.enter_context(nc.sbuf_tensor(name, [P] + shape, dt))

        def sem(name):
            return stack.enter_context(nc.semaphore(name))

        ps_t = [stack.enter_context(nc.psum_tensor(f"ps_t{i}", [P, HALF], F32)) for i in range(2)]
        ps_mid = [stack.enter_context(nc.psum_tensor(f"ps_mid{i}", [P, HALF], F32)) for i in range(2)]
        ps_low = [stack.enter_context(nc.psum_tensor(f"ps_low{i}", [P, 2, HALF], F32)) for i in range(2)]

        X = sb("X", [B, J2, D])
        S = sb("S", [B, J2, D])
        Y = sb("Y", [B, J2, D])
        XH = sb("XH", [B, J2, D])
        KT = sb("KT", [B, C2, N])
        V = sb("V", [B, J2, D + 2])
        XT = sb("XT", [2, C2, K])
        PR = sb("PR", [4, J2, K])
        GT = sb("GT", [4, C2, K])
        wn = sb("wn", [5, C2, D])
        wt = sb("wt", [3, C2, D])
        Wkq = sb("Wkq", [C2, D])
        Wvu = sb("Wvu", [C2, D])
        wf = sb("wf", [2 * H * D // P])
        w3 = sb("w3", [2 * H * D // P], F16)
        below = sb("below", [CHUNK])
        colv = sb("colv", [NCOL])
        rowv = sb("rowv", [NROW])
        vbias = sb("vbias", [J2, D])
        lnb_out = sb("lnb_out", [J2, D])
        ident = sb("ident", [P])
        ones = sb("ones", [P])
        bcol = sb("bcol", [C2, P])
        lnbh = sb("lnbh", [HT], F16)
        lnbl = sb("lnbl", [HT], F16)
        lnb_row = sb("lnb_row", [D])
        ckv = sb("ckv", [4, 1])
        kgain = sb("kgain", [C2])
        kbias = sb("kbias", [C2])
        b1fold = sb("b1fold", [C2])
        absum = sb("absum", [2])
        thr = sb("thr", [2, 2])
        nmax = sb("nmax", [B, J2])
        rsum = sb("rsum", [B, J2])
        rinv = sb("rinv", [B, J2])
        cinv = sb("cinv", [B, J2, 1])
        mhalf = sb("mhalf", [J2])

        cond_row = rowv[:, ROW_COND:].rearrange("p (b d) -> p b d", b=B)

        def row(name):
            return rowv[:, ROW[name]:ROW[name] + D]

        def col(name, c):
            return colv[:, COL[name] + c:COL[name] + c + 1]

        WK, WV, WU, W1, W2 = range(5)
        TK, TQ, TV = range(3)
        W1g = wt[:, TK]
        WfT = w3[:, 0:C2 * H].rearrange("p (c h) -> p c h", c=C2)
        WpT = w3[:, C2 * H:].rearrange("p (t d) -> p t d", t=HT)
        Gf = KT[:, :, :, :].rearrange("p b c n -> p (b c n)")[:, 0:2 * H].rearrange("p (r h) -> p r h", r=2)
        GC = KT[:, :, :, :].rearrange("p b c n -> p (b c n)")[:, 2 * H:4 * H].rearrange("p (r h) -> p r h", r=2)
        XR = PR[:, 0:2]
        vf = V[:, :, :, :].rearrange("p b j d -> p (b j d)")

        def halves(at, n):
            return vf[:, at:at + n // 2].bitcast(F16)

        gsum = sb("gsum", [2, 2])
        qsum = sb("qsum", [2, 2])
        gneg = sb("gneg", [2])
        grstd = sb("grstd", [2, 3])

        XTh = halves(0, 2 * C2 * N).rearrange("p (u c k) -> p u c k", u=2, c=C2)
        XTl = halves(C2 * N, 2 * C2 * N).rearrange("p (u c k) -> p u c k", u=2, c=C2)
        GTh = halves(2 * C2 * N, 2 * HT * P).rearrange("p (r t k) -> p r t k", r=2, t=HT)
        GTl = halves(2 * C2 * N + HT * P, 2 * HT * P).rearrange("p (r t k) -> p r t k", r=2, t=HT)

        class Norm:

            def __init__(self, name, slots=B, tiles=J2, applied=None):
                self.tiles = tiles
                self.slots = slots
                self.applied = applied
                self.st = sb(f"{name}_st", [slots, tiles, 2, 6])
                self.mv = sb(f"{name}_mv", [slots, tiles, 2])
                self.ve = sb(f"{name}_ve", [slots, tiles])
                self.nm = sb(f"{name}_nm", [slots, tiles])
                self.ab = sb(f"{name}_ab", [slots, 2, tiles])
                self.stats_done = sem(f"{name}_stats_done")
                self.moments = sem(f"{name}_moments")
                self.chain = sem(f"{name}_chain")
                self.coef = sem(f"{name}_coef")


        ctx_in_sem = [sem(f"ctx_in{u}") for u in range(2)]
        x_in_sem = [sem(f"x_in{u}") for u in range(2)]
        cols_in = sem("cols_in")
        bu_in = sem("bu_in")
        rows_in = sem("rows_in")
        wkq_in = sem("wkq_in")
        wvu_in = sem("wvu_in")
        mlp_in = sem("mlp_in")
        ffn_in = sem("ffn_in")
        stored = sem("stored")
        consts = sem("consts")
        c_ready = sem("c_ready")
        w_prod = sem("w_prod")
        w_fold = sem("w_fold")
        cv_spread = sem("cv_spread")
        sig_ready = sem("sig_ready")
        xc_ready = sem("xc_ready")
        xq_ready = sem("xq_ready")
        xm_ready = sem("xm_ready")
        xf_ready = sem("xf_ready")
        x_scaled = sem("x_scaled")
        p_scaled = sem("p_scaled")
        y_ready = sem("y_ready")
        s_shifted = sem("s_shifted")
        t_ready = sem("t_ready")
        t_copied = sem("t_copied")
        mid_ready = sem("mid_ready")
        mid_read = sem("mid_read")
        low_ready = sem("low_ready")
        low_read = sem("low_read")
        max_ready = sem("max_ready")
        rinv_ready = sem("rinv_ready")
        attn_ready = sem("attn_ready")
        cinv_ready = sem("cinv_ready")
        mag_ready = sem("mag_ready")
        thr_ready = sem("thr_ready")
        below_ready = sem("below_ready")
        tern_ready = sem("tern_ready")
        lnb_parts = sem("lnb_parts")
        lnb_prod = sem("lnb_prod")
        lnb_copied = sem("lnb_copied")
        x1_ready = sem("x1_ready")
        x1_shifted = sem("x1_shifted")
        xth_ready = sem("xth_ready")
        xtl_ready = sem("xtl_ready")
        f1_ready = sem("f1_ready")
        gelu_done = sem("gelu_done")
        gneg_ready = sem("gneg_ready")
        sq_done = sem("sq_done")
        g_chain = sem("g_chain")
        grstd_ready = sem("grstd_ready")
        gc_done = sem("gc_done")
        tg_ready = sem("tg_ready")
        gth_ready = sem("gth_ready")
        gtl_ready = sem("gtl_ready")
        o_ready = sem("o_ready")
        o_done = sem("o_done")
        dve_held, pool_held = sem("dve_held"), sem("pool_held")

        class Norm:

            def __init__(self, name, slots, used, per_item):
                self.slots = slots
                self.used, self.per_item = used, per_item
                self.st = sb(f"{name}_st", [slots, J2, 6])
                self.mv = sb(f"{name}_mv", [slots, J2, 2])
                self.ve = sb(f"{name}_ve", [slots, J2])
                self.nm = sb(f"{name}_nm", [slots, J2])
                self.ab = sb(f"{name}_ab", [slots, 2, J2])
                self.stats_done = sem(f"{name}_stats_done")
                self.moments = sem(f"{name}_moments")
                self.chain = sem(f"{name}_chain")
                self.coef = sem(f"{name}_coef")

        lnc, lnx = Norm("lnc", 2, xc_ready, 1), Norm("lnx", 2, y_ready, 2)
        lni, lnf = Norm("lni", 2, xq_ready, 1), Norm("lnf", 2, xf_ready, 2)
        lnq, lnm, lnp = (Norm(n, B, None, 0) for n in ("lnq", "lnm", "lnp"))

        x_v = x.rearrange("b (p j) d -> b p (j d)", j=J2)
        c_v = ctx_in.rearrange("b (p j) d -> b p (j d)", j=J2)
        o_v = out.rearrange("b (p j) d -> b p (j d)", j=J2)

        def flat(t, b):
            return t[:, b].rearrange("p j d -> p (j d)")

        def early(n):
            return isinstance(n, int) and n < 2

        def pairs(eng, step, lo=1, hi=B // 2 - 1):
            for b in range(2 * lo):
                step(b, b % 2, b, None)
            with eng.Fori(lo, hi) as i:
                for u in range(2):
                    step(2 * i + u, u, None, None)
            for b in range(2 * hi, B):
                step(b, b % 2, None, b)

        def in_rounds(eng, step):
            for s in range(LEAD):
                step(0, s, False)
            with eng.Fori(0, ROUNDS - 1) as t:
                for s in range(LEAD, STEPS + LEAD):
                    step(t, s, False)
            for s in range(LEAD, STEPS + LEAD):
                step(ROUNDS - 1, s, True)

        def item(t, s, lag, last):
            i = s - lag
            if i < 0 or (last and i >= STEPS):
                return None
            return t + (i // STEPS), (i // B) % 2, i % B

        def ring(t, half, b):
            return t * STEPS + (B + half * B + b)

        T_FFN = B + ROUNDS * STEPS

        def bn_rows(dve, ln, at, tiles):
            dve.sem_inc(dve_held, 1)
            for j in range(J2):
                dve.bn_stats(ln.st[:, at, j], tiles[:, j]).then_inc(ln.stats_done, 1)

        def bn_sum(dve, ln, n, at):
            if ln.slots == 2 and not early(n):
                dve.wait_ge(ln.coef, n - 1)
            dve.wait_ge(ln.stats_done, J2 * n + J2)
            dve.sem_inc(dve_held, 1)
            for j in range(J2):
                dve.bn_aggr(ln.mv[:, at, j], ln.st[:, at, j]).then_inc(ln.moments, 1)

        def ln_coef(pool, ln, n, at, shift=True):
            if ln.slots == 2 and not early(n):
                pool.wait_ge(ln.used, (n - 1) * ln.per_item)
            pool.wait_ge(ln.moments, J2 * n + J2)
            pool.sem_inc(pool_held, 1)
            pool.tensor_scalar(ln.ve[:, at], ln.mv[:, at, :, 1], LN_EPS, None, ALU.add).then_inc(ln.chain, 1)
            if not shift:
                pool.wait_ge(ln.chain, n + 1)
                pool.tensor_tensor(ln.ab[:, at, 0], ln.ve[:, at], mhalf[:], ALU.pow).then_inc(ln.coef, 1)
                return
            pool.tensor_scalar(ln.nm[:, at], ln.mv[:, at, :, 0], -1.0, None, ALU.mult).then_inc(ln.chain, 1)
            pool.wait_ge(ln.chain, n * 3 + 2)
            pool.tensor_tensor(ln.ab[:, at, 0], ln.ve[:, at], mhalf[:], ALU.pow).then_inc(ln.chain, 1)
            pool.wait_ge(ln.chain, n * 3 + 3)
            pool.tensor_tensor(ln.ab[:, at, 1], ln.nm[:, at], ln.ab[:, at, 0], ALU.mult).then_inc(ln.coef, 1)

        def ln_apply(act, ln, n, at, src, dst, ready):
            act.wait_ge(ln.coef, n + 1)
            for j in range(J2):
                last = act.activation(dst[:, j], src[:, j], ACT.Identity,
                                      bias=ln.ab[:, at, 1, j:j + 1], scale=ln.ab[:, at, 0, j:j + 1])
            last.then_inc(ready, 1)

        def centre_gain(dve, ln, n, at, src, dst, gain, done):
            dve.wait_ge(ln.moments, J2 * n + J2)
            for j in range(J2):
                dve.scalar_tensor_tensor(out=dst[:, j], in0=src[:, j], scalar=ln.mv[:, at, j, 0:1], in1=gain,
                                         op0=ALU.subtract, op1=ALU.mult).then_inc(done, 1)

        def rstd_shift(dve, ln, n, at, src, dst, shift, done, ready):
            dve.wait_ge(ln.coef, n + 1)
            dve.wait_ge(done, J2 * n + J2)
            for j in range(J2):
                dve.scalar_tensor_tensor(out=dst[:, j], in0=src[:, j], scalar=ln.ab[:, at, 0, j:j + 1], in1=shift,
                                         op0=ALU.mult, op1=ALU.add).then_inc(ready, 1)

        def blocks_t(pe, dst, src):
            for c in range(C2):
                for j in range(J2):
                    last = pe.transpose(dst[:, c * K + j * P:c * K + (j + 1) * P],
                                        src[:, j, c * P:(c + 1) * P], ident[:])
            last.then_inc(t_ready, 1)

        def product(pe, dst, lhs_t, rhs, n=D):
            for m in range(2):
                for c in range(2):
                    last = pe.matmul(dst(m), lhs_t[:, c, m * P:(m + 1) * P], rhs[:, c, 0:n],
                                     start=(c == 0), stop=(c == 1))
            return last

        def side(ps):
            return lambda m: ps[:, m * D:(m + 1) * D]

        def copy_xt(act, s, u):
            act.wait_ge(t_ready, s + 1)
            act.wait_ge(mid_ready, s + 1)
            act.activation(XT[:, u].rearrange("p c k -> p (c k)"), ps_t[u][:], ACT.Copy).then_inc(t_copied, 1)

        FOLD_CK, FOLD_CV, FOLD_KQ, FOLD_K, FOLD_V, FOLD_ALL = 1, 2, 4, 8, 12, 15
        TERN_ALL = (ROUNDS - 1) * B

        block = stack.enter_context(nc.Block())

        @block.sync
        def _(sp):
            for b in range(B):
                for dst, src, s in ((S, c_v, ctx_in_sem[b % 2]), (X, x_v, x_in_sem[b % 2])):
                    if b >= 2:
                        sp.wait_ge(s, 16 * (b // 2))
                    sp.dma_start(flat(dst, b), src[b]).then_inc(s, 16)
            sp.dma_start(wn[:, W1:W2 + 1].rearrange("p w c d -> p w (c d)"),
                         w_nat[3:5].rearrange("w p n -> p w n")).then_inc(mlp_in, 16)
            sp.dma_start(rowv[:, ROWS_EARLY:], rows[ROWS_EARLY:].rearrange("(a n) -> a n", a=1)
                         .broadcast_to([P, NROW - ROWS_EARLY])).then_inc(rows_in, 16)
            sp.dma_start(wf[:, 0:C2 * H], w_fc_t).then_inc(ffn_in, 16)
            sp.dma_start(wf[:, C2 * H:], w_proj_t).then_inc(ffn_in, 16)
            with sp.Fori(0, B) as b:
                sp.wait_ge(o_done, 2 * b + 2)
                sp.dma_start(o_v[b], flat(X, b)).then_inc(stored, 16)
            sp.wait_ge(stored, 16 * B)

        @block.gpsimd
        def _(pool):
            pool.memset(ident[:], 0.0).then_inc(consts, 1)
            pool.memset(ones[:], 1.0).then_inc(consts, 1)
            pool.memset(mhalf[:], -0.5).then_inc(consts, 1)
            pool.memset(V[:, :, :, D:D + 1], 1.0).then_inc(consts, 1)
            pool.wait_ge(consts, 1)
            pool.affine_select(out=ident[:], in_=ident[:], compare_op=ALU.not_equal, fill=1.0, base=0,
                               pattern=[[-1, P]], channel_multiplier=1).then_inc(consts, 1)
            pool.wait_ge(consts, 5)

            def prologue(b, u, first, last):
                if last is None or last < B - 1:
                    ln_coef(pool, lnc, b + 1, 1 - u)
                ln_coef(pool, lnx, b, u, shift=False)
                if first is None or first >= 1:
                    ln_coef(pool, lni, b - 1, 1 - u)

            ln_coef(pool, lnc, 0, 0)
            pairs(pool, prologue)
            ln_coef(pool, lni, B - 1, 1)

            def rounds(t, s, last):
                if s == 0:
                    pool.wait_ge(rows_in, 16)
                    for b in range(B):
                        pool.tensor_tensor(cond_row[:, b], cond_row[:, b], row("b2"), ALU.add).then_inc(c_ready, 1)
                    pool.wait_ge(c_ready, B)
                if it := item(t, s, 3, last):
                    r, half, b = it
                    if half == 0:
                        ln_coef(pool, lnm, r * B + b, b)
                    else:
                        ln_coef(pool, lnp, r * B + b, b, shift=False)
                if it := item(t, s, -3, last):
                    r, half, b = it
                    if half == 0 and s + 3 >= STEPS:
                        ln_coef(pool, lnq, (r - 1) * B + b, b)
                if it := item(t, s, 4, last):
                    r, half, b = it
                    if half == 0:
                        pool.wait_ge(xm_ready, r * B + (b + 1))
                        for j in range(J2):
                            pool.tensor_tensor(S[:, b, j], S[:, b, j], cond_row[:, b], ALU.add)\
                                .then_inc(s_shifted, 1)

            in_rounds(pool, rounds)

            def x1(b):
                pool.wait_ge(y_ready, ROUNDS * J2 * B + J2 * b + J2)
                pool.sem_inc(pool_held, 1)
                pool.tensor_tensor(flat(X, b), flat(X, b), flat(Y, b), ALU.add).then_inc(x1_ready, 1)

            def rstd_g(r, rt):
                if not early(r):
                    pool.wait_ge(o_done, r - 1)
                pool.wait_ge(sq_done, 2 * r + 2)
                pool.sem_inc(pool_held, 1)
                pool.tensor_scalar(grstd[:, rt, 0:1], qsum[:, rt, 0:1], qsum[:, rt, 1:2], H * LN_EPS,
                                   ALU.add, ALU.add).then_inc(g_chain, 1)
                pool.wait_ge(g_chain, 2 * r + 1)
                pool.tensor_tensor(grstd[:, rt, 1:2], grstd[:, rt, 0:1], mhalf[:, 0:1], ALU.pow).then_inc(g_chain, 1)
                pool.wait_ge(g_chain, 2 * r + 2)
                pool.sem_inc(pool_held, 1)
                pool.tensor_scalar(grstd[:, rt, 2:3], grstd[:, rt, 1:2], float(H) ** 0.5, None, ALU.mult)\
                    .then_inc(grstd_ready, 1)

            x1(0)
            ln_coef(pool, lnf, 0, 0, shift=False)
            x1(1)
            pool.wait_ge(lnb_copied, 3)

            def ffn(b, u, first, last):
                if last is None or last < B - 1:
                    ln_coef(pool, lnf, b + 1, 1 - u, shift=False)
                if last is None:
                    x1(b + 2)
                pool.wait_ge(xf_ready, 2 * b + 2)
                pool.sem_inc(pool_held, 1)
                pool.tensor_tensor(flat(X, b), flat(X, b), lnb_out[:].rearrange("p j d -> p (j d)"),
                                   ALU.add).then_inc(x1_shifted, 1)
                for rt in range(2):
                    rstd_g(2 * b + rt, rt)

            pairs(pool, ffn)

        @block.scalar
        def _(act):
            def load(dst, src, s):
                act.dma_start(dst, src).then_inc(s, 16)

            load(wn[:, WK].rearrange("p c d -> p (c d)"), w_nat[0], wkq_in)
            load(colv[:], cols, cols_in)
            load(wt[:, TK:TQ + 1].rearrange("p w c d -> p w (c d)"), w_tr[0:2].rearrange("w p n -> p w n"), wkq_in)
            load(wn[:, WV:WU + 1].rearrange("p w c d -> p w (c d)"), w_nat[1:3].rearrange("w p n -> p w n"), wvu_in)
            load(wt[:, TV].rearrange("p c d -> p (c d)"), w_tr[2], wvu_in)
            load(rowv[:, 0:ROWS_EARLY], rows[0:ROWS_EARLY].rearrange("(a n) -> a n", a=1)
                 .broadcast_to([P, ROWS_EARLY]), bu_in)
            act.sem_inc(t_copied, RING)
            act.sem_inc(mid_read, 2 * RING)

            ln_apply(act, lnc, 0, 0, S[:, 0], XR[:, 0], xc_ready)
            act.wait_ge(bu_in, 16)
            act.activation(row("q_logsig"), row("q_logsig"), ACT.Exp).then_inc(sig_ready, 1)

            def prologue(b, u, first, last):
                copy_xt(act, b, u)
                if last is None or last < B - 1:
                    ln_apply(act, lnc, b + 1, 1 - u, S[:, b + 1], XR[:, 1 - u], xc_ready)
                act.wait_ge(w_fold, FOLD_K)
                act.wait_ge(mid_ready, b + (1 + RING))
                for c in range(C2):
                    act.activation(KT[:, b, c], ps_mid[u][:, c * N:(c + 1) * N], ACT.Identity,
                                   bias=kbias[:, c:c + 1], scale=kgain[:, c:c + 1]).then_inc(mid_read, 1)
                if first is None or first >= 1:
                    ln_apply(act, lni, b - 1, 1 - u, Y[:, b - 1], XH[:, b - 1], xq_ready)

            pairs(act, prologue)
            ln_apply(act, lni, B - 1, 1, Y[:, B - 1], XH[:, B - 1], xq_ready)

            def rounds(t, s, last):
                if it := item(t, s, 0, last):
                    r, half, b = it
                    copy_xt(act, ring(r, half, b), b % 2)
                if s in (1, 2) and isinstance(t, int) and t == 0 and not last:
                    act.wait_ge(ffn_in, 32)
                    raw = wf[:, (s - 1) * C2 * H:s * C2 * H]
                    act.activation(w3[:, (s - 1) * C2 * H:s * C2 * H], raw, ACT.Abs,
                                   accum_out=absum[:, s - 1:s]).then_inc(mag_ready, 1)
                if it := item(t, s, -2, last):
                    r, half, b = it
                    if half == 0 and s + 2 >= STEPS:
                        ln_apply(act, lnq, (r - 1) * B + b, b, Y[:, b], XH[:, b], xq_ready)
                if it := item(t, s, 4, last):
                    r, half, b = it
                    if half == 0:
                        ln_apply(act, lnm, r * B + b, b, S[:, b], XH[:, b], xm_ready)
                if it := item(t, s, 1, last):
                    r, half, b = it
                    n = ring(r, half, b)
                    dst = PR if half == 0 else GT
                    if half == 0:
                        act.wait_ge(max_ready, r * B + (b + 1))
                    else:
                        act.wait_ge(mid_ready, n + (1 + RING))
                    if b >= 4:
                        act.wait_ge(low_ready, n - 4 + 1)
                    for j in range(2):
                        src = ps_mid[b % 2][:, j * K:(j + 1) * K]
                        if half == 0:
                            act.activation(dst[:, b % 4, j], src, ACT.Exp, bias=nmax[:, b, j:j + 1],
                                           accum_out=rsum[:, b, j:j + 1]).then_inc(mid_read, 1)
                        else:
                            act.activation(dst[:, b % 4, j], src, ACT.Gelu, bias=b1fold[:, j:j + 1])\
                               .then_inc(mid_read, 1)

            in_rounds(act, rounds)

            def copy_high(b, u):
                act.wait_ge(t_ready, b + (T_FFN + 1))
                if not early(b):
                    act.wait_ge(f1_ready, 4 * b - 4)
                act.activation(XTh[:, u].rearrange("p c k -> p (c k)"), ps_t[0][:], ACT.Copy).then_inc(xth_ready, 1)

            def gelu_half(r, rt, h):
                act.wait_ge(f1_ready, 2 * r + (h + 1))
                if not early(r):
                    act.wait_ge(gc_done, 2 * r - 2)
                act.activation(Gf[:, rt, h * HALF:(h + 1) * HALF], ps_mid[h][:], ACT.Gelu,
                               accum_out=gsum[:, rt, h:h + 1]).then_inc(gelu_done, 1)

            def square_half(r, rt, h):
                act.wait_ge(gneg_ready, r + 1)
                if not early(r):
                    act.wait_ge(grstd_ready, r - 1)
                act.activation(flat(XH, 2 * rt + h), Gf[:, rt, h * HALF:(h + 1) * HALF], ACT.Square, bias=gneg[:, rt:rt + 1],
                               accum_out=qsum[:, rt, h:h + 1]).then_inc(sq_done, 1)

            def high_half(r, rt, h):
                act.wait_ge(tg_ready, 2 * r + (h + 1))
                if not early(r):
                    act.wait_ge(o_ready, r - 1)
                act.activation(GTh[:, rt, 4 * h:4 * h + 4].rearrange("p t k -> p (t k)"), ps_low[rt][:, h],
                               ACT.Copy).then_inc(gth_ready, 1)

            copy_high(0, 0)

            def ffn(b, u, first, last):
                for rt in range(2):
                    r = 2 * b + rt
                    gelu_half(r, rt, 0)
                    gelu_half(r, rt, 1)
                    if rt == 1 or first != 0:
                        high_half(r - 1, 1 - rt, 0)
                        high_half(r - 1, 1 - rt, 1)
                    square_half(r, rt, 0)
                    square_half(r, rt, 1)
                    if rt == 0 and (last is None or last < B - 1):
                        copy_high(b + 1, 1 - u)

            pairs(act, ffn)
            for h in range(2):
                high_half(2 * B - 1, 1, h)

        @block.vector
        def _(dve):
            dve.sem_inc(low_read, 2 * RING)

            def stats_c(b, u):
                dve.wait_ge(ctx_in_sem[u], 8 * b + (16 - 8 * u))
                bn_rows(dve, lnc, u, S[:, b])
                bn_sum(dve, lnc, b, u)

            stats_c(0, 0)
            dve.wait_ge(cols_in, 16)
            dve.wait_ge(w_prod, 1)
            dve.tensor_tensor(ckv[:, 0:2, 0], ps_low[0][:, 0, 0:2], colv[:, COL["bk"]:COL["bk"] + 2],
                              ALU.add).then_inc(w_fold, 1)
            stats_c(1, 1)
            dve.wait_ge(w_prod, 3)
            dve.tensor_tensor(ckv[:, 2:4, 0], ps_low[0][:, 1, 0:2], colv[:, COL["bv"]:COL["bv"] + 2],
                              ALU.add).then_inc(w_fold, 1)
            for c in range(C2):
                dve.tensor_scalar(Wkq[:, c], ps_mid[0][:, c * D:(c + 1) * D], col("lnkv_g", c), None,
                                  ALU.mult).then_inc(w_fold, 1)
            for c in range(C2):
                dve.tensor_scalar(kgain[:, c:c + 1], col("lnq_g", c), LOGIT_SCALE, None, ALU.mult).then_inc(w_fold, 1)
            dve.wait_ge(w_prod, 4)
            for c in range(C2):
                dve.tensor_scalar(kbias[:, c:c + 1], ps_low[1][:, 0, c:c + 1], col("lnq_g", c), LOGIT_SCALE,
                                  ALU.mult, ALU.mult).then_inc(w_fold, 1)
            dve.wait_ge(w_fold, FOLD_CV)
            dve.wait_ge(consts, 5)
            for c in range(C2):
                dve.tensor_scalar(bcol[:, c], ones[:], ckv[:, 2 + c], None, ALU.mult).then_inc(cv_spread, 1)
            dve.wait_ge(w_prod, 5)
            for c in range(C2):
                dve.tensor_scalar(Wvu[:, c], ps_mid[1][:, c * D:(c + 1) * D], col("lnkv_g", c), None,
                                  ALU.mult).then_inc(w_fold, 1)
            dve.wait_ge(bu_in, 16)
            dve.wait_ge(w_prod, 6)
            for j in range(J2):
                dve.tensor_tensor(vbias[:, j], ps_low[1][:, 1, 0:D], row("bu"), ALU.add).then_inc(w_fold, 1)
            dve.wait_ge(sig_ready, 1)

            def prologue(b, u, first, last):
                if last is None:
                    stats_c(b + 2, u)
                dve.wait_ge(x_in_sem[u], 8 * b + (16 - 8 * u))
                bn_rows(dve, lnx, u, X[:, b])
                bn_sum(dve, lnx, b, u)
                if first is None or first >= 1:
                    first_slots(b - 1, 1 - u)
                centre_gain(dve, lnx, b, u, X[:, b], XH[:, b], row("q_logsig"), x_scaled)
                dve.wait_ge(low_ready, b + 1)
                if isinstance(b, int) and b == 0:
                    dve.wait_ge(w_fold, FOLD_V)
                dve.tensor_tensor(V[:, b, :, 0:D], ps_low[u][:, 0].rearrange("p (j d) -> p j d", j=J2), vbias[:],
                                  ALU.add).then_inc(low_read, 2)

            def first_slots(b, u):
                rstd_shift(dve, lnx, b, u, XH[:, b], Y[:, b], row("q_mu"), x_scaled, y_ready)
                dve.wait_ge(y_ready, J2 * b + J2)
                bn_rows(dve, lni, u, Y[:, b])
                bn_sum(dve, lni, b, u)

            pairs(dve, prologue)
            first_slots(B - 1, 1)

            dve.wait_ge(mlp_in, 16)
            for c in range(C2):
                dve.tensor_scalar(W1g[:, c], wn[:, W1, c], col("lnm_g", c), None, ALU.mult).then_inc(w_fold, 1)
            dve.wait_ge(w_prod, 7)
            dve.tensor_tensor(b1fold[:], ps_low[0][:, 1, 0:2], colv[:, COL["b1"]:COL["b1"] + 2],
                              ALU.add).then_inc(w_fold, 1)
            dve.tensor_copy(lnbh[:], colv[:, COL_LNB:COL_LNB + HT]).then_inc(lnb_parts, 1)
            dve.wait_ge(lnb_parts, 1)
            dve.tensor_tensor(lnbl[:], colv[:, COL_LNB:COL_LNB + HT], lnbh[:], ALU.subtract).then_inc(lnb_parts, 1)

            def rounds(t, s, last):
                head = isinstance(t, int) and not last
                at_q = item(t, s, -3, last)
                at_q = at_q if at_q and at_q[1] == 0 and s + 3 >= STEPS else None
                if it := item(t, s, 2, last):
                    r, half, b = it
                    if half == 0:
                        dve.wait_ge(mid_read, ring(r, half, b) * 2 + (2 + 2 * RING))
                        dve.reciprocal(rinv[:, b], rsum[:, b]).then_inc(rinv_ready, 1)
                if it := item(t, s, 4, last):
                    r, half, b = it
                    if half == 1:
                        rstd_shift(dve, lnp, r * B + b, b, XH[:, b], Y[:, b], row("lnp_b"), p_scaled, y_ready)
                if it := item(t, s, 2, last):
                    r, half, b = it
                    if half == 0:
                        dve.wait_ge(rinv_ready, r * B + (b + 1))
                        for j in range(J2):
                            dve.tensor_scalar(PR[:, b % 4, j], PR[:, b % 4, j], rinv[:, b, j:j + 1], EPS_ATTN,
                                              ALU.mult, ALU.add).then_inc(attn_ready, 1)
                if at_q:
                    r, half, b = at_q
                    dve.wait_ge(y_ready, r * (J2 * B) + (J2 * b + J2))
                    bn_rows(dve, lnq, b, Y[:, b])
                if it := item(t, s, 1, last):
                    r, half, b = it
                    if half == 0:
                        dve.wait_ge(mid_ready, ring(r, half, b) + (1 + RING))
                        dve.tensor_reduce(nmax[:, b], ps_mid[b % 2][:].rearrange("p (j k) -> p j k", j=J2), AX.X,
                                          ALU.max, negate=True).then_inc(max_ready, 1)
                if at_q:
                    r, half, b = at_q
                    bn_sum(dve, lnq, (r - 1) * B + b, b)
                chunk = None
                if not head and not last and s % 2 == 0:
                    k = (s - LEAD) // 2
                    chunk = (t * B + k) * CHUNK
                    cut = bass.ds(chunk, CHUNK)
                if it := item(t, s, 3, last):
                    r, half, b = it
                    n = ring(r, half, b)
                    ps = ps_low[b % 2]
                    dve.wait_ge(low_ready, n + 1)
                    if half == 0:
                        dve.reciprocal(cinv[:, b], ps[:, :, D:D + 1]).then_inc(cinv_ready, 1)
                        if chunk is not None:
                            ternary_below(t * B + k, cut)
                        dve.wait_ge(cinv_ready, r * B + (b + 1))
                        for j in range(J2):
                            dve.scalar_tensor_tensor(out=S[:, b, j], in0=ps[:, j, 0:D], scalar=cinv[:, b, j],
                                                     in1=Y[:, b, j], op0=ALU.mult, op1=ALU.add).then_inc(low_read, 1)
                        ln = lnm
                    else:
                        dve.wait_ge(s_shifted, r * (J2 * B) + (J2 * b + J2))
                        dve.tensor_tensor(flat(S, b), ps[:, 0], flat(S, b), ALU.add).then_inc(low_read, 2)
                        if chunk is not None:
                            ternary_below(t * B + k, cut)
                        ln = lnp
                    dve.wait_ge(low_read, 2 * n + (2 + 2 * RING))
                    bn_rows(dve, ln, b, S[:, b])
                    if chunk is not None:
                        ternary_above(t * B + k, cut, (t * B + k))
                    bn_sum(dve, ln, r * B + b, b)
                    if half == 1:
                        centre_gain(dve, lnp, r * B + b, b, S[:, b], XH[:, b], row("lnp_g"), p_scaled)
                if head and s == LEAD - 1:
                    dve.tensor_scalar(thr[:, 0], ps_low[0][:, 1, D + 2:D + 4], 1.0 / (H * D), EPS_TERNARY,
                                      ALU.mult, ALU.add).then_inc(thr_ready, 1)
                    dve.wait_ge(thr_ready, 1)
                    dve.tensor_scalar(thr[:, 1], thr[:, 0], -0.5, None, ALU.mult).then_inc(thr_ready, 1)
                    dve.wait_ge(thr_ready, 2)
                    dve.tensor_scalar(thr[:, 0], thr[:, 1], -1.0, None, ALU.mult).then_inc(thr_ready, 1)
                    dve.wait_ge(thr_ready, 3)

            def ternary_below(n, cut):
                dve.tensor_scalar(below[:], wf[:, cut], thr_now(1, n), None, ALU.is_lt).then_inc(below_ready, 1)

            def ternary_above(n, cut, done):
                dve.wait_ge(below_ready, n + 1)
                dve.scalar_tensor_tensor(out=w3[:, cut], in0=wf[:, cut], scalar=thr_now(0, n), in1=below[:],
                                         op0=ALU.is_gt, op1=ALU.subtract).then_inc(tern_ready, 1)

            def thr_now(sign, n):
                return thr[:, sign, bass.ds(n_pass[0], 1)]

            n_pass = [None]

            def rounds_with_pass(t, s, last):
                n_pass[0] = t
                rounds(t, s, last)

            in_rounds(dve, rounds_with_pass)

            def stats_f(b, u):
                dve.wait_ge(x1_ready, b + 1)
                bn_rows(dve, lnf, u, X[:, b])
                bn_sum(dve, lnf, b, u)

            def apply_f(b, u):
                dve.wait_ge(lnf.coef, b + 1)
                if not early(b):
                    dve.wait_ge(t_ready, b + (T_FFN - 1))
                for j in range(J2):
                    dve.tensor_scalar(XR[:, u, j], X[:, b, j], lnf.mv[:, u, j, 0:1], lnf.ab[:, u, 0, j:j + 1],
                                      ALU.subtract, ALU.mult).then_inc(xf_ready, 1)

            def low_parts(b, u):
                dve.wait_ge(xth_ready, b + 1)
                if not early(b):
                    dve.wait_ge(f1_ready, 4 * b - 4)
                dve.tensor_tensor(XTl[:, u].rearrange("p c k -> p (c k)"), ps_t[0][:],
                                  XTh[:, u].rearrange("p c k -> p (c k)"), ALU.subtract).then_inc(xtl_ready, 1)

            def centre(r, rt):
                dve.wait_ge(gelu_done, 2 * r + 2)
                if not early(r):
                    dve.wait_ge(sq_done, 2 * r - 2)
                dve.tensor_scalar(gneg[:, rt:rt + 1], gsum[:, rt, 0:1], gsum[:, rt, 1:2], -1.0 / H,
                                  ALU.add, ALU.mult).then_inc(gneg_ready, 1)
                if not early(r):
                    dve.wait_ge(tg_ready, 2 * r - 2)
                dve.wait_ge(gneg_ready, r + 1)
                for h in range(2):
                    dve.scalar_tensor_tensor(out=GC[:, rt, h * HALF:(h + 1) * HALF],
                                             in0=Gf[:, rt, h * HALF:(h + 1) * HALF], scalar=gneg[:, rt:rt + 1],
                                             in1=rowv[:, ROW_LNW + h * HALF:ROW_LNW + (h + 1) * HALF],
                                             op0=ALU.add, op1=ALU.mult).then_inc(gc_done, 1)

            def low_half(r, rt, h):
                dve.wait_ge(gth_ready, 2 * r + (h + 1))
                if not early(r):
                    dve.wait_ge(o_ready, r - 1)
                dve.tensor_tensor(GTl[:, rt, 4 * h:4 * h + 4].rearrange("p t k -> p (t k)"), ps_low[rt][:, h],
                                  GTh[:, rt, 4 * h:4 * h + 4].rearrange("p t k -> p (t k)"), ALU.subtract)\
                   .then_inc(gtl_ready, 1)

            def result(b, r, rt):
                dve.wait_ge(o_ready, r + 1)
                dve.wait_ge(grstd_ready, r + 1)
                dve.wait_ge(x1_shifted, b + 1)
                dve.scalar_tensor_tensor(out=X[:, b, rt], in0=ps_t[1][:, 0:D], scalar=grstd[:, rt, 2:3],
                                         in1=X[:, b, rt], op0=ALU.mult, op1=ALU.add).then_inc(o_done, 1)

            stats_f(0, 0)
            dve.wait_ge(lnb_prod, 1)
            dve.tensor_copy(lnb_row[0:1, :], ps_mid[0][0:1, 0:D]).then_inc(lnb_copied, 1)
            apply_f(0, 0)
            stats_f(1, 1)
            dve.wait_ge(lnb_prod, 2)
            for j in range(J2):
                dve.tensor_copy(lnb_out[:, j], ps_mid[1][:, 0:D]).then_inc(lnb_copied, 1)
            low_parts(0, 0)

            def ffn(b, u, first, last):
                for rt in range(2):
                    r = 2 * b + rt
                    if rt == 0 and (last is None or last < B - 1):
                        apply_f(b + 1, 1 - u)
                    if rt == 1 and last is None:
                        stats_f(b + 2, u)
                    centre(r, rt)
                    if rt == 1 or first != 0:
                        low_half(r - 1, 1 - rt, 0)
                        low_half(r - 1, 1 - rt, 1)
                    if rt == 0 and (last is None or last < B - 1):
                        low_parts(b + 1, 1 - u)
                    if first != 0:
                        result(b - 1, r - 2, rt)

            pairs(dve, ffn)
            result(B - 1, 2 * B - 2, 0)
            for h in range(2):
                low_half(2 * B - 1, 1, h)
            result(B - 1, 2 * B - 1, 1)

        @block.tensor
        def _(pe):
            pe.sem_inc(mid_ready, RING)
            pe.wait_ge(wkq_in, 32)
            pe.wait_ge(cols_in, 16)

            def column(dst, w, v):
                for m in range(C2):
                    for c in range(C2):
                        last = pe.matmul(dst[:, m:m + 1], w[:, c, m * P:(m + 1) * P], v(c),
                                         start=(c == 0), stop=(c == C2 - 1))
                return last

            column(ps_low[0][:, 0], wn[:, WK], lambda c: col("lnkv_b", c)).then_inc(w_prod, 1)
            last = product(pe, side(ps_mid[0]), wt[:, TK], wt[:, TQ])
            pe.wait_ge(wvu_in, 32)
            column(ps_low[0][:, 1], wn[:, WV], lambda c: col("lnkv_b", c)).then_inc(w_prod, 2)
            pe.wait_ge(w_fold, FOLD_CK)
            column(ps_low[1][:, 0], wt[:, TQ], lambda c: ckv[:, c]).then_inc(w_prod, 1)
            product(pe, side(ps_mid[1]), wt[:, TV], wn[:, WU]).then_inc(w_prod, 1)
            pe.wait_ge(cv_spread, 2)
            for c in range(C2):
                last = pe.matmul(ps_low[1][:, 1, 0:D], bcol[:, c], wn[:, WU, c], start=(c == 0), stop=(c == C2 - 1))
            last.then_inc(w_prod, 1)
            pe.wait_ge(consts, 5)

            def context_t(b, u):
                pe.wait_ge(xc_ready, b + 1)
                pe.wait_ge(t_copied, b + 1)
                blocks_t(pe, ps_t[u], XR[:, u])

            def keys_values(b, u):
                pe.wait_ge(t_copied, b + (1 + RING))
                if isinstance(b, int) and b == 0:
                    pe.wait_ge(w_fold, FOLD_V)
                pe.wait_ge(low_read, 2 * b + 2)
                product(pe, side(ps_low[u][:, 0]), XT[:, u], Wvu).then_inc(low_ready, 1)
                pe.wait_ge(mid_read, 2 * b + 2)
                product(pe, side(ps_mid[u]), Wkq, XT[:, u]).then_inc(mid_ready, 1)

            context_t(0, 0)

            def prologue(b, u, first, last):
                if last is None or last < B - 1:
                    context_t(b + 1, 1 - u)
                keys_values(b, u)

            pairs(pe, prologue)

            pe.wait_ge(mlp_in, 16)
            pe.wait_ge(low_read, 2 * (B - 1) + 2 * RING)
            column(ps_low[0][:, 1], wn[:, W1], lambda c: col("lnm_b", c)).then_inc(w_prod, 1)

            def rounds(t, s, last):
                if it := item(t, s, 0, last):
                    r, half, b = it
                    if half == 0:
                        pe.wait_ge(xq_ready, r * B + (b + 1))
                    else:
                        pe.wait_ge(xm_ready, r * B + (b + 1))
                    pe.wait_ge(t_copied, ring(r, half, b) + 1)
                    blocks_t(pe, ps_t[b % 2], XH[:, b])
                if it := item(t, s, 1, last):
                    r, half, b = it
                    n = ring(r, half, b)
                    pe.wait_ge(t_copied, n + (1 + RING))
                    pe.wait_ge(mid_read, 2 * n + 2)
                    if half == 0:
                        product(pe, side(ps_mid[b % 2]), KT[:, b], XT[:, b % 2]).then_inc(mid_ready, 1)
                    else:
                        product(pe, side(ps_mid[b % 2]), W1g, XT[:, b % 2]).then_inc(mid_ready, 1)
                if it := item(t, s, 3, last):
                    r, half, b = it
                    n = ring(r, half, b)
                    ps = ps_low[b % 2]
                    if half == 0:
                        pe.wait_ge(attn_ready, r * (J2 * B) + (J2 * b + J2))
                        pe.wait_ge(low_read, 2 * n + 2)
                        if isinstance(t, int) and s == 3 and not last:
                            pe.wait_ge(w_fold, FOLD_ALL)
                        if isinstance(t, int) and s == LEAD - 1 and not last:
                            pe.wait_ge(mag_ready, 2)
                            pe.matmul(ps[:, 1, D + 2:D + 4], ones[:], absum[:], start=True, stop=True)
                        product(pe, lambda m: ps[:, m, 0:D + 1], PR[:, b % 4], V[:, b], D + 1).then_inc(low_ready, 1)
                    else:
                        pe.wait_ge(mid_read, 2 * n + (2 + 2 * RING))
                        pe.wait_ge(low_read, 2 * n + 2)
                        product(pe, side(ps[:, 0]), GT[:, b % 4], wn[:, W2]).then_inc(low_ready, 1)

            in_rounds(pe, rounds)

            def rows_t(b, u):
                pe.wait_ge(xf_ready, 2 * b + 2)
                if isinstance(b, int) and b == 0:
                    pe.wait_ge(t_copied, T_FFN + RING)
                else:
                    pe.wait_ge(xtl_ready, b)
                blocks_t(pe, ps_t[0], XR[:, u])

            def fc(b, u, r, rt):
                if rt == 0:
                    pe.wait_ge(xtl_ready, b + 1)
                for h in range(2):
                    if isinstance(r, int) and r == 0:
                        pe.wait_ge(lnb_copied, 3)
                    else:
                        pe.wait_ge(gelu_done, 2 * r + (h - 1))
                    parts = [(c, part) for c in range(C2) for part in (XTh, XTl)]
                    for k, (c, part) in enumerate(parts):
                        last = pe.matmul(ps_mid[h][:], part[:, u, c, rt * P:(rt + 1) * P],
                                         WfT[:, c, h * HALF:(h + 1) * HALF], start=(k == 0), stop=(k == 3))
                    last.then_inc(f1_ready, 1)

            def hidden_t(r, rt):
                for h in range(2):
                    pe.wait_ge(gc_done, 2 * r + (h + 1))
                    if not early(r):
                        pe.wait_ge(gtl_ready, 2 * r + (h - 3))
                    for k in range(4):
                        last = pe.transpose(ps_low[rt][:, h, k * P:(k + 1) * P],
                                            GC[:, rt, (4 * h + k) * P:(4 * h + k + 1) * P], ident[:])
                    last.then_inc(tg_ready, 1)

            def proj(r, rt):
                pe.wait_ge(gtl_ready, 2 * r + 2)
                if not (isinstance(r, int) and r == 0):
                    pe.wait_ge(o_done, r)
                for k in range(HT):
                    for part in (GTh, GTl):
                        last = pe.matmul(ps_t[1][:, 0:D], part[:, rt, k], WpT[:, k],
                                         start=(k == 0 and part is GTh), stop=(k == HT - 1 and part is GTl))
                last.then_inc(o_ready, 1)

            pe.wait_ge(tern_ready, TERN_ALL)
            pe.wait_ge(lnb_parts, 2)
            pe.wait_ge(mid_read, 2 * T_FFN + 2 * RING)
            for k in range(HT):
                for part in (lnbh, lnbl):
                    last = pe.matmul(ps_mid[0][0:1, 0:D], part[:, k:k + 1], WpT[:, k],
                                     start=(k == 0 and part is lnbh), stop=(k == HT - 1 and part is lnbl))
            last.then_inc(lnb_prod, 1)
            rows_t(0, 0)
            pe.wait_ge(lnb_copied, 1)
            pe.matmul(ps_mid[1][:, 0:D], ones[0:1, :], lnb_row[0:1, :], start=True, stop=True).then_inc(lnb_prod, 1)

            def ffn(b, u, first, last):
                for rt in range(2):
                    r = 2 * b + rt
                    fc(b, u, r, rt)
                    if rt == 1 or first != 0:
                        hidden_t(r - 1, 1 - rt)
                    if rt == 0 and (last is None or last < B - 1):
                        rows_t(b + 1, 1 - u)
                    if first != 0:
                        proj(r - 2, rt)

            pairs(pe, ffn)
            hidden_t(2 * B - 1, 1)
            proj(2 * B - 2, 0)
            proj(2 * B - 1, 1)


def kernel(**inputs):
    import numpy as np
    import concourse.bacc as bacc
    from concourse.bass_utils import run_bass_kernel_spmd

    g = {k: np.asarray(v) for k, v in inputs.items()}
    xc = {k[len("L0_xcond_"):]: v for k, v in g.items() if k.startswith("L0_xcond_")}

    def tiles(w):
        r, c = w.shape
        return w.reshape(r // P, P, c).transpose(1, 0, 2).reshape(P, -1)

    def columns(v):
        return v.reshape(-1, P).T

    arrays = {
        "x": g["x"],
        "ctx": g["ctx_1024"],
        "w_nat": np.stack([tiles(xc[n]) for n in ("wk", "wv", "wu", "w1", "w2")]),
        "w_tr": np.stack([tiles(xc[n].T) for n in ("wk", "wq", "wv")]),
        "w_fc_t": tiles(g["L0_ffn_W_fc"].T),
        "w_proj_t": tiles(g["L0_ffn_W_proj"].T),
        "cols": np.concatenate([columns(xc[n]) for n in COL] + [columns(g["L0_ffn_ln_b"])], axis=1),
        "rows": np.concatenate([xc[n].reshape(-1) for n in ROW] + [g["L0_ffn_ln_w"], g["cond_1024"].reshape(-1)]),
    }
    arrays = {k: np.ascontiguousarray(v) for k, v in arrays.items()}
    nc = bacc.Bacc("TRN2", target_bir_lowering=False, num_devices=1)
    aps = [nc.dram_tensor(k, v.shape, mybir.dt.from_np(v.dtype), kind="ExternalInput").ap() for k, v in arrays.items()]
    out = nc.dram_tensor("out", g["x"].shape, F32, kind="ExternalOutput").ap()
    build(nc, *aps, out)
    r = run_bass_kernel_spmd(nc, [arrays], core_ids=[0])
    return r.results[0]["out"]
```

```python
from contextlib import ExitStack

import concourse.bass as bass
from concourse import mybir

F32 = mybir.dt.float32
F16 = mybir.dt.float16
ALU = mybir.AluOpType
ACT = mybir.ActivationFunctionType
AX = mybir.AxisListType

B, N, K, D, H = 8, 256, 256, 256, 1024
ROUNDS = 3
P = 128
C2 = D // P
J2 = N // P
HT = H // P
HALF = 512
LOGIT_SCALE = float(D) ** 0.5
EPS_ATTN = 1e-8
LN_EPS = 1e-5
EPS_TERNARY = 1e-6
STEPS = 2 * B
LEAD = 7
WARM_UP = 11
SUM_STEP = 5
CHUNK = 2 * H * D // P // (ROUNDS - 1) // B
RING = 2

COL = {name: C2 * i for i, name in enumerate(
    ["lnkv_g", "lnkv_b", "lnq_g", "lnm_g", "lnm_b", "bk", "bv", "b1"])}
COL_LNB = C2 * len(COL)
NCOL = COL_LNB + HT
ROW = {name: D * i for i, name in enumerate(["bu", "q_mu", "q_logsig", "lnp_g", "lnp_b", "b2"])}
ROWS_EARLY = 3 * D
ROW_LNW = D * len(ROW)
ROW_COND = ROW_LNW + H
NROW = ROW_COND + B * D


def build(nc, x, ctx_in, w_nat, w_tr, w_fc_t, w_proj_t, cols, rows, out):
    with ExitStack() as stack:
        def sb(name, shape, dt=F32):
            return stack.enter_context(nc.sbuf_tensor(name, [P] + shape, dt))

        def sem(name):
            return stack.enter_context(nc.semaphore(name))

        ps_t = [stack.enter_context(nc.psum_tensor(f"ps_t{i}", [P, HALF], F32)) for i in range(2)]
        ps_mid = [stack.enter_context(nc.psum_tensor(f"ps_mid{i}", [P, HALF], F32)) for i in range(2)]
        ps_low = [stack.enter_context(nc.psum_tensor(f"ps_low{i}", [P, 2, HALF], F32)) for i in range(2)]

        X = sb("X", [B, J2, D])
        S = sb("S", [B, J2, D])
        Y = sb("Y", [B, J2, D])
        XH = sb("XH", [B, J2, D])
        KT = sb("KT", [B, C2, N])
        V = sb("V", [B, J2, D + 2])
        XT = sb("XT", [2, C2, K])
        PR = sb("PR", [4, J2, K])
        GT = sb("GT", [4, C2, K])
        wn = sb("wn", [5, C2, D])
        wt = sb("wt", [3, C2, D])
        Wkq = sb("Wkq", [C2, D])
        Wvu = sb("Wvu", [C2, D])
        wf = sb("wf", [2 * H * D // P])
        w3 = sb("w3", [2 * H * D // P], F16)
        below = sb("below", [2, CHUNK])
        colv = sb("colv", [NCOL])
        rowv = sb("rowv", [NROW])
        vbias = sb("vbias", [J2, D])
        lnb_out = sb("lnb_out", [J2, D])
        ident = sb("ident", [P])
        ones = sb("ones", [P])
        bcol = sb("bcol", [C2, P])
        lnbh = sb("lnbh", [HT], F16)
        lnbl = sb("lnbl", [HT], F16)
        lnb_row = sb("lnb_row", [D])
        ckv = sb("ckv", [4, 1])
        kgain = sb("kgain", [C2])
        kbias = sb("kbias", [C2])
        b1fold = sb("b1fold", [C2])
        absum = sb("absum", [2])
        thr = sb("thr", [2, 2])
        nmax = sb("nmax", [B, J2])
        rsum = sb("rsum", [B, J2])
        rinv = sb("rinv", [B, J2])
        cinv = sb("cinv", [B, J2, 1])
        mhalf = sb("mhalf", [J2])

        cond_row = rowv[:, ROW_COND:].rearrange("p (b d) -> p b d", b=B)

        def row(name):
            return rowv[:, ROW[name]:ROW[name] + D]

        def col(name, c):
            return colv[:, COL[name] + c:COL[name] + c + 1]

        WK, WV, WU, W1, W2 = range(5)
        TK, TQ, TV = range(3)
        W1g = wt[:, TK]
        WfT = w3[:, 0:C2 * H].rearrange("p (c h) -> p c h", c=C2)
        WpT = w3[:, C2 * H:].rearrange("p (t d) -> p t d", t=HT)
        Gf = KT[:, :, :, :].rearrange("p b c n -> p (b c n)")[:, 0:2 * H].rearrange("p (r h) -> p r h", r=2)
        GC = KT[:, :, :, :].rearrange("p b c n -> p (b c n)")[:, 2 * H:4 * H].rearrange("p (r h) -> p r h", r=2)
        XR = PR[:, 0:2]
        vf = V[:, :, :, :].rearrange("p b j d -> p (b j d)")

        def halves(at, n):
            return vf[:, at:at + n // 2].bitcast(F16)

        gsum = sb("gsum", [2, 2])
        qsum = sb("qsum", [2, 2])
        gneg = sb("gneg", [2])
        grstd = sb("grstd", [2, 3])

        XTh = halves(0, 2 * C2 * N).rearrange("p (u c k) -> p u c k", u=2, c=C2)
        XTl = halves(C2 * N, 2 * C2 * N).rearrange("p (u c k) -> p u c k", u=2, c=C2)
        GTh = halves(2 * C2 * N, 2 * HT * P).rearrange("p (r t k) -> p r t k", r=2, t=HT)
        GTl = halves(2 * C2 * N + HT * P, 2 * HT * P).rearrange("p (r t k) -> p r t k", r=2, t=HT)

        ctx_in_sem = [sem(f"ctx_in{u}") for u in range(2)]
        x_in_sem = [sem(f"x_in{u}") for u in range(2)]
        cols_in = sem("cols_in")
        bu_in = sem("bu_in")
        rows_in = sem("rows_in")
        wkq_in = sem("wkq_in")
        wk_in = sem("wk_in")
        wvu_in = sem("wvu_in")
        mlp_in = sem("mlp_in")
        ffn_in = sem("ffn_in")
        stored = sem("stored")
        consts = sem("consts")
        c_ready = sem("c_ready")
        w_prod = sem("w_prod")
        w_fold = sem("w_fold")
        cv_spread = sem("cv_spread")
        sig_ready = sem("sig_ready")
        xc_ready = sem("xc_ready")
        xq_ready = sem("xq_ready")
        xm_ready = sem("xm_ready")
        xf_ready = sem("xf_ready")
        x_scaled = sem("x_scaled")
        x_unit = sem("x_unit")
        y_half = sem("y_half")
        xp_ready = sem("xp_ready")
        p_scaled = sem("p_scaled")
        y_ready = sem("y_ready")
        x_shifted = sem("x_shifted")
        s_shifted = sem("s_shifted")
        t_ready = sem("t_ready")
        t_copied = sem("t_copied")
        mid_ready = sem("mid_ready")
        mid_read = sem("mid_read")
        low_ready = sem("low_ready")
        low_read = sem("low_read")
        max_ready = sem("max_ready")
        rinv_ready = sem("rinv_ready")
        attn_ready = sem("attn_ready")
        cinv_ready = sem("cinv_ready")
        mag_ready = sem("mag_ready")
        thr_ready = sem("thr_ready")
        below_ready = sem("below_ready")
        tern_ready = sem("tern_ready")
        lnb_parts = sem("lnb_parts")
        lnb_prod = sem("lnb_prod")
        lnb_copied = sem("lnb_copied")
        x1_ready = sem("x1_ready")
        x1_shifted = sem("x1_shifted")
        xth_ready = sem("xth_ready")
        xtl_ready = sem("xtl_ready")
        f1_ready = sem("f1_ready")
        gelu_done = sem("gelu_done")
        gneg_ready = sem("gneg_ready")
        sq_done = sem("sq_done")
        g_chain = sem("g_chain")
        grstd_ready = sem("grstd_ready")
        gc_done = sem("gc_done")
        tg_ready = sem("tg_ready")
        gth_ready = sem("gth_ready")
        gtl_ready = sem("gtl_ready")
        o_ready = sem("o_ready")
        o_done = sem("o_done")
        dve_held, pool_held = sem("dve_held"), sem("pool_held")

        class Norm:

            def __init__(self, name, slots, used, per_item, base=0):
                self.slots = slots
                self.used, self.per_item = used, per_item
                self.base = base
                self.st = sb(f"{name}_st", [slots, J2, 6])
                self.mv = sb(f"{name}_mv", [slots, J2, 2])
                self.ve = sb(f"{name}_ve", [slots, J2])
                self.nm = sb(f"{name}_nm", [slots, J2])
                self.ab = sb(f"{name}_ab", [slots, 2, J2])
                self.stats_done = sem(f"{name}_stats_done")
                self.moments = sem(f"{name}_moments")
                self.chain = sem(f"{name}_chain")
                self.coef = sem(f"{name}_coef")

        lnc, lnx = Norm("lnc", 2, xc_ready, 1), Norm("lnx", 2, x_unit, 1)
        lni, lnf = Norm("lni", 2, xq_ready, 1, RING), Norm("lnf", 2, xf_ready, 2)
        lnq, lnm, lnp = (Norm(n, B, None, 0) for n in ("lnq", "lnm", "lnp"))

        x_v = x.rearrange("b (p j) d -> b p (j d)", j=J2)
        c_v = ctx_in.rearrange("b (p j) d -> b p (j d)", j=J2)
        o_v = out.rearrange("b (p j) d -> b p (j d)", j=J2)

        def flat(t, b):
            return t[:, b].rearrange("p j d -> p (j d)")

        def early(n):
            return isinstance(n, int) and n < 2

        def pairs(eng, step, start=0, lo=1, hi=B // 2 - 1):
            for b in range(start, 2 * lo):
                step(b, b % 2, b, None)
            with eng.Fori(lo, hi) as i:
                for u in range(2):
                    step(2 * i + u, u, None, None)
            for b in range(2 * hi, B):
                step(b, b % 2, None, b)

        def in_rounds(eng, step):
            for s in range(LEAD):
                step(0, s, False)
            with eng.Fori(0, ROUNDS - 1) as t:
                for s in range(LEAD, STEPS + LEAD):
                    step(t, s, False)
            for s in range(LEAD, STEPS + LEAD):
                step(ROUNDS - 1, s, True)

        def item(t, s, lag, last):
            i = s - lag
            if i < 0 or (last and i >= STEPS):
                return None
            return t + (i // STEPS), (i // B) % 2, i % B

        def ring(t, half, b):
            return t * STEPS + (B + half * B + b)

        T_FFN = B + ROUNDS * STEPS

        FFN_STEP = STEPS + 1

        def bn_rows(dve, ln, at, tiles):
            dve.sem_inc(dve_held, 1)
            for j in range(J2):
                dve.bn_stats(ln.st[:, at, j], tiles[:, j]).then_inc(ln.stats_done, 1)

        def bn_sum(dve, ln, n, at):
            if ln.slots == 2 and not early(n):
                dve.wait_ge(ln.coef, n + (ln.base - 1))
            dve.wait_ge(ln.stats_done, J2 * n + J2)
            dve.sem_inc(dve_held, 1)
            for j in range(J2):
                dve.bn_aggr(ln.mv[:, at, j], ln.st[:, at, j]).then_inc(ln.moments, 1)

        def ln_coef(pool, ln, n, at, shift=True):
            if ln.slots == 2 and not early(n):
                pool.wait_ge(ln.used, n * ln.per_item + (ln.base - ln.per_item))
            pool.wait_ge(ln.moments, J2 * n + J2)
            pool.sem_inc(pool_held, 1)
            pool.tensor_scalar(ln.ve[:, at], ln.mv[:, at, :, 1], LN_EPS, None, ALU.add).then_inc(ln.chain, 1)
            if not shift:
                pool.wait_ge(ln.chain, n + 1)
                pool.tensor_tensor(ln.ab[:, at, 0], ln.ve[:, at], mhalf[:], ALU.pow).then_inc(ln.coef, 1)
                return
            pool.tensor_scalar(ln.nm[:, at], ln.mv[:, at, :, 0], -1.0, None, ALU.mult).then_inc(ln.chain, 1)
            pool.wait_ge(ln.chain, n * 3 + 2)
            pool.tensor_tensor(ln.ab[:, at, 0], ln.ve[:, at], mhalf[:], ALU.pow).then_inc(ln.chain, 1)
            pool.wait_ge(ln.chain, n * 3 + 3)
            pool.tensor_tensor(ln.ab[:, at, 1], ln.nm[:, at], ln.ab[:, at, 0], ALU.mult).then_inc(ln.coef, 1)

        def ln_apply(act, ln, n, at, src, dst, ready):
            act.wait_ge(ln.coef, n + (1 + ln.base))
            for j in range(J2):
                last = act.activation(dst[:, j], src[:, j], ACT.Identity,
                                      bias=ln.ab[:, at, 1, j:j + 1], scale=ln.ab[:, at, 0, j:j + 1])
            last.then_inc(ready, 1)

        def centre_gain(dve, ln, n, at, src, dst, gain, done):
            dve.wait_ge(ln.moments, J2 * n + J2)
            for j in range(J2):
                dve.scalar_tensor_tensor(out=dst[:, j], in0=src[:, j], scalar=ln.mv[:, at, j, 0:1], in1=gain,
                                         op0=ALU.subtract, op1=ALU.mult).then_inc(done, 1)

        def blocks_t(pe, dst, src):
            for c in range(C2):
                for j in range(J2):
                    last = pe.transpose(dst[:, c * K + j * P:c * K + (j + 1) * P],
                                        src[:, j, c * P:(c + 1) * P], ident[:])
            last.then_inc(t_ready, 1)

        def product(pe, dst, lhs_t, rhs, n=D):
            for m in range(2):
                for c in range(2):
                    last = pe.matmul(dst(m), lhs_t[:, c, m * P:(m + 1) * P], rhs[:, c, 0:n],
                                     start=(c == 0), stop=(c == 1))
            return last

        def side(ps):
            return lambda m: ps[:, m * D:(m + 1) * D]

        def copy_xt(act, s, u):
            act.wait_ge(t_ready, s + 1)
            act.wait_ge(mid_ready, s + 1)
            act.activation(XT[:, u].rearrange("p c k -> p (c k)"), ps_t[u][:], ACT.Copy).then_inc(t_copied, 1)

        FOLD_CK, FOLD_CV, FOLD_K, FOLD_V, FOLD_ALL = 3, 8, 10, 12, 15
        TERN_ALL = (ROUNDS - 1) * B

        block = stack.enter_context(nc.Block())

        @block.sync
        def _(sp):
            def load(dst, src, s, b):
                if b >= 2:
                    sp.wait_ge(s[b % 2], 16 * (b // 2))
                sp.dma_start(flat(dst, b), src[b]).then_inc(s[b % 2], 16)

            load(S, c_v, ctx_in_sem, 0)
            load(S, c_v, ctx_in_sem, 1)
            sp.wait_ge(wk_in, 16)
            for b in range(B):
                load(X, x_v, x_in_sem, b)
                if b + 2 < B:
                    load(S, c_v, ctx_in_sem, b + 2)
            sp.dma_start(wn[:, W1:W2 + 1].rearrange("p w c d -> p w (c d)"),
                         w_nat[3:5].rearrange("w p n -> p w n")).then_inc(mlp_in, 16)
            sp.dma_start(rowv[:, ROWS_EARLY:], rows[ROWS_EARLY:].rearrange("(a n) -> a n", a=1)
                         .broadcast_to([P, NROW - ROWS_EARLY])).then_inc(rows_in, 16)
            sp.dma_start(wf[:, 0:C2 * H], w_fc_t).then_inc(ffn_in, 16)
            sp.dma_start(wf[:, C2 * H:], w_proj_t).then_inc(ffn_in, 16)
            with sp.Fori(0, B) as b:
                sp.wait_ge(o_done, 2 * b + 2)
                sp.dma_start(o_v[b], flat(X, b)).then_inc(stored, 16)
            sp.wait_ge(stored, 16 * B)

        @block.gpsimd
        def _(pool):
            pool.memset(ident[:], 0.0).then_inc(consts, 1)
            pool.memset(ones[:], 1.0).then_inc(consts, 1)
            pool.memset(mhalf[:], -0.5).then_inc(consts, 1)
            pool.memset(V[:, :, :, D:D + 1], 1.0).then_inc(consts, 1)
            pool.wait_ge(consts, 1)
            pool.affine_select(out=ident[:], in_=ident[:], compare_op=ALU.not_equal, fill=1.0, base=0,
                               pattern=[[-1, P]], channel_multiplier=1).then_inc(consts, 1)
            pool.wait_ge(consts, 5)
            pool.sem_inc(lni.coef, RING)

            def prologue(b, u, first, last):
                if last is None:
                    ln_coef(pool, lnc, b + 2, u)
                if first is None:
                    ln_coef(pool, lni, b - 2, u)
                if last is None or last < B - 1:
                    ln_coef(pool, lnx, b + 1, 1 - u, shift=False)
                pool.wait_ge(x_unit, b + 1)
                pool.sem_inc(pool_held, 1)
                pool.tensor_tensor(Y[:, b, 1], XH[:, b, 1], row("q_mu"), ALU.add).then_inc(y_ready, J2)

            ln_coef(pool, lnc, 0, 0)
            ln_coef(pool, lnc, 1, 1)
            ln_coef(pool, lnx, 0, 0, shift=False)
            pairs(pool, prologue)

            def rstd_g(r, rt):
                if not early(r):
                    pool.wait_ge(o_done, r - 1)
                pool.wait_ge(sq_done, 2 * r + 2)
                pool.sem_inc(pool_held, 1)
                pool.tensor_scalar(grstd[:, rt, 0:1], qsum[:, rt, 0:1], qsum[:, rt, 1:2], H * LN_EPS,
                                   ALU.add, ALU.add).then_inc(g_chain, 1)
                pool.wait_ge(g_chain, 2 * r + 1)
                pool.tensor_tensor(grstd[:, rt, 1:2], grstd[:, rt, 0:1], mhalf[:, 0:1], ALU.pow).then_inc(g_chain, 1)
                pool.wait_ge(g_chain, 2 * r + 2)
                pool.sem_inc(pool_held, 1)
                pool.tensor_scalar(grstd[:, rt, 2:3], grstd[:, rt, 1:2], float(H) ** 0.5, None, ALU.mult)\
                    .then_inc(grstd_ready, 1)

            def ffn(b, u, rt, last=None):
                if rt == 0:
                    rstd_g(2 * b - 1, 1)
                else:
                    if last is None:
                        ln_coef(pool, lnf, b + 2, u, shift=False)
                    rstd_g(2 * b, 0)
                    pool.wait_ge(xf_ready, 2 * b + 2)
                    pool.sem_inc(pool_held, 1)
                    pool.tensor_tensor(flat(X, b), flat(X, b), lnb_out[:].rearrange("p j d -> p (j d)"),
                                       ALU.add).then_inc(x1_shifted, 1)

            def into_ffn(s):
                if s == FFN_STEP + 1:
                    pool.wait_ge(lnb_copied, 3)
                    ffn(0, 0, 1)

            def norm_coefs(t, s, last):
                if it := item(t, s, 3, last):
                    r, half, b = it
                    ln_coef(pool, lnp if half else lnm, r * B + b, b)

            def rounds(t, s, last):
                if s == 2 and isinstance(t, int) and not last:
                    pool.wait_ge(rows_in, 16)
                    for b in range(B):
                        pool.tensor_tensor(cond_row[:, b], cond_row[:, b], row("b2"), ALU.add).then_inc(c_ready, 1)
                    pool.wait_ge(c_ready, B)
                if isinstance(t, int) and not last and s < 2:
                    ln_coef(pool, lni, B - 2 + s, s)
                if last:
                    if s in (STEPS - 2, STEPS):
                        k = (s - STEPS + 2) // 2
                        ln_coef(pool, lnf, k, k, shift=False)
                    norm_coefs(t, s, last)
                if it := item(t, s, 4 if last else 5, last):
                    r, half, b = it
                    if half == 1:
                        pool.wait_ge(p_scaled, r * (J2 * B) + (J2 * b + J2))
                        if last:
                            pool.wait_ge(x_shifted, J2 * b + J2)
                            for j in range(J2):
                                pool.tensor_tensor(X[:, b, j], X[:, b, j], XH[:, b, j], ALU.add)\
                                    .then_inc(x1_ready, 1)
                        else:
                            for j in range(J2):
                                pool.tensor_tensor(Y[:, b, j], XH[:, b, j], row("lnp_b"), ALU.add)\
                                    .then_inc(y_ready, 1)
                if it := item(t, s, -2, last):
                    r, half, b = it
                    if half == 0 and s + 2 >= STEPS:
                        ln_coef(pool, lnq, (r - 1) * B + b, b)
                if not last:
                    norm_coefs(t, s, last)
                if it := item(t, s, 4, last):
                    r, half, b = it
                    if half == 0:
                        pool.wait_ge(xm_ready, r * B + (b + 1))
                        for j in range(J2):
                            pool.tensor_tensor(S[:, b, j], S[:, b, j], cond_row[:, b], ALU.add)\
                                .then_inc(s_shifted, 1)
                if last:
                    into_ffn(s)

            in_rounds(pool, rounds)

            def both(b, u, first, last):
                ffn(b, u, 0, last)
                ffn(b, u, 1, last)

            pairs(pool, both, start=1)
            rstd_g(2 * B - 1, 1)

        @block.scalar
        def _(act):
            def load(dst, src, s):
                act.dma_start(dst, src).then_inc(s, 16)

            load(wt[:, TK:TQ + 1].rearrange("p w c d -> p w (c d)"), w_tr[0:2].rearrange("w p n -> p w n"), wkq_in)
            load(colv[:], cols, cols_in)
            load(wn[:, WK].rearrange("p c d -> p (c d)"), w_nat[0], wk_in)
            load(wn[:, WV:WU + 1].rearrange("p w c d -> p w (c d)"), w_nat[1:3].rearrange("w p n -> p w n"), wvu_in)
            load(wt[:, TV].rearrange("p c d -> p (c d)"), w_tr[2], wvu_in)
            load(rowv[:, 0:ROWS_EARLY], rows[0:ROWS_EARLY].rearrange("(a n) -> a n", a=1)
                 .broadcast_to([P, ROWS_EARLY]), bu_in)
            act.sem_inc(t_copied, RING)
            act.sem_inc(mid_read, 2 * RING)
            act.sem_inc(xq_ready, RING)

            ln_apply(act, lnc, 0, 0, S[:, 0], XR[:, 0], xc_ready)
            act.wait_ge(bu_in, 16)
            act.activation(row("q_logsig"), row("q_logsig"), ACT.Exp).then_inc(sig_ready, 1)

            copy_xt(act, 0, 0)
            ln_apply(act, lnc, 1, 1, S[:, 1], XR[:, 1], xc_ready)

            def prologue(b, u, first, last):
                if last is None or last < B - 1:
                    copy_xt(act, b + 1, 1 - u)
                if last is None:
                    ln_apply(act, lnc, b + 2, u, S[:, b + 2], XR[:, u], xc_ready)
                act.wait_ge(lnx.coef, b + 1)
                act.wait_ge(x_scaled, J2 * b + J2)
                act.activation(XH[:, b, 1], XH[:, b, 1], ACT.Copy, scale=lnx.ab[:, u, 0, 1:2]).then_inc(x_unit, 1)
                if first is None:
                    ln_apply(act, lni, b - 2, u, Y[:, b - 2], XH[:, b - 2], xq_ready)
                act.wait_ge(w_fold, FOLD_K)
                act.wait_ge(mid_ready, b + (1 + RING))
                for c in range(C2):
                    act.activation(KT[:, b, c], ps_mid[u][:, c * N:(c + 1) * N], ACT.Identity,
                                   bias=kbias[:, c:c + 1], scale=kgain[:, c:c + 1]).then_inc(mid_read, 1)

            pairs(act, prologue)

            def copy_high(b, u):
                act.wait_ge(t_ready, b + (T_FFN + 1))
                if not early(b):
                    act.wait_ge(f1_ready, 4 * b - 4)
                act.activation(XTh[:, u].rearrange("p c k -> p (c k)"), ps_t[0][:], ACT.Copy).then_inc(xth_ready, 1)

            def gelu_half(r, rt, h):
                act.wait_ge(f1_ready, 2 * r + (h + 1))
                if not early(r):
                    act.wait_ge(gc_done, 2 * r - 2)
                act.activation(Gf[:, rt, h * HALF:(h + 1) * HALF], ps_mid[h][:], ACT.Gelu,
                               accum_out=gsum[:, rt, h:h + 1]).then_inc(gelu_done, 1)

            def square_half(r, rt, h):
                act.wait_ge(gneg_ready, r + 1)
                if not early(r):
                    act.wait_ge(grstd_ready, r - 1)
                act.activation(flat(XH, 2 * rt + h), Gf[:, rt, h * HALF:(h + 1) * HALF], ACT.Square,
                               bias=gneg[:, rt:rt + 1], accum_out=qsum[:, rt, h:h + 1]).then_inc(sq_done, 1)

            def high_half(r, rt, h):
                act.wait_ge(tg_ready, 2 * r + (h + 1))
                if not early(r):
                    act.wait_ge(o_ready, r - 1)
                act.activation(GTh[:, rt, 4 * h:4 * h + 4].rearrange("p t k -> p (t k)"), ps_low[rt][:, h],
                               ACT.Copy).then_inc(gth_ready, 1)

            def ffn(b, u, rt, last=None):
                r = 2 * b + rt
                gelu_half(r, rt, 0)
                gelu_half(r, rt, 1)
                if not (isinstance(r, int) and r == 0):
                    high_half(r - 1, 1 - rt, 0)
                    high_half(r - 1, 1 - rt, 1)
                square_half(r, rt, 0)
                square_half(r, rt, 1)
                if rt == 0 and (last is None or last < B - 1):
                    copy_high(b + 1, 1 - u)

            def into_ffn(s):
                if s == STEPS - 1:
                    copy_high(0, 0)
                if s in (FFN_STEP, FFN_STEP + 1):
                    ffn(0, 0, s - FFN_STEP)

            def apply_norms(t, s, last):
                if it := item(t, s, 4, last):
                    r, half, b = it
                    if half == 0:
                        ln_apply(act, lnm, r * B + b, b, S[:, b], XH[:, b], xm_ready)
                    else:
                        ln_apply(act, lnp, r * B + b, b, S[:, b], XH[:, b], xp_ready)

            def rounds(t, s, last):
                if it := item(t, s, 0, last):
                    r, half, b = it
                    copy_xt(act, ring(r, half, b), b % 2)
                if s < 2 and isinstance(t, int) and not last:
                    ln_apply(act, lni, B - 2 + s, s, Y[:, B - 2 + s], XH[:, B - 2 + s], xq_ready)
                if s in (3, 4) and isinstance(t, int) and not last:
                    act.wait_ge(ffn_in, 32)
                    k = s - 3
                    act.activation(w3[:, k * C2 * H:(k + 1) * C2 * H], wf[:, k * C2 * H:(k + 1) * C2 * H], ACT.Abs,
                                   accum_out=absum[:, k:k + 1]).then_inc(mag_ready, 1)
                if it := item(t, s, -1, last):
                    r, half, b = it
                    if half == 0 and s + 1 >= STEPS:
                        ln_apply(act, lnq, (r - 1) * B + b, b, Y[:, b], XH[:, b], xq_ready)
                if not last:
                    apply_norms(t, s, last)
                if it := item(t, s, 1, last):
                    r, half, b = it
                    n = ring(r, half, b)
                    dst = PR if half == 0 else GT
                    if half == 0:
                        act.wait_ge(max_ready, r * B + (b + 1))
                    else:
                        act.wait_ge(mid_ready, n + (1 + RING))
                    if b >= 4:
                        act.wait_ge(low_ready, n - 4 + 1)
                    for j in range(2):
                        src = ps_mid[b % 2][:, j * K:(j + 1) * K]
                        if half == 0:
                            act.activation(dst[:, b % 4, j], src, ACT.Exp, bias=nmax[:, b, j:j + 1],
                                           accum_out=rsum[:, b, j:j + 1]).then_inc(mid_read, 1)
                        else:
                            act.activation(dst[:, b % 4, j], src, ACT.Gelu, bias=b1fold[:, j:j + 1])\
                               .then_inc(mid_read, 1)
                if last:
                    apply_norms(t, s, last)
                if last:
                    into_ffn(s)

            in_rounds(act, rounds)

            def both(b, u, first, last):
                ffn(b, u, 0, last)
                ffn(b, u, 1, last)

            pairs(act, both, start=1)
            for h in range(2):
                high_half(2 * B - 1, 1, h)

        @block.vector
        def _(dve):
            dve.sem_inc(low_read, 2 * RING)

            def rows_c(b, u):
                dve.wait_ge(ctx_in_sem[u], 8 * b + (16 - 8 * u))
                bn_rows(dve, lnc, u, S[:, b])

            def rows_x(b, u):
                dve.wait_ge(x_in_sem[u], 8 * b + (16 - 8 * u))
                bn_rows(dve, lnx, u, X[:, b])

            def rows_y(b, u):
                dve.wait_ge(y_half, b + 1)
                dve.wait_ge(y_ready, J2 * b + J2)
                bn_rows(dve, lni, u, Y[:, b])

            for b in range(2):
                rows_c(b, b)
                bn_sum(dve, lnc, b, b)
            dve.wait_ge(cols_in, 16)
            dve.wait_ge(w_prod, 1)
            for c in range(C2):
                dve.tensor_scalar(Wkq[:, c], ps_mid[0][:, c * D:(c + 1) * D], col("lnkv_g", c), None,
                                  ALU.mult).then_inc(w_fold, 1)
            dve.wait_ge(w_prod, 2)
            dve.tensor_tensor(ckv[:, 0:2, 0], ps_low[0][:, 0, 0:2], colv[:, COL["bk"]:COL["bk"] + 2],
                              ALU.add).then_inc(w_fold, 1)
            for c in range(C2):
                dve.tensor_scalar(kgain[:, c:c + 1], col("lnq_g", c), LOGIT_SCALE, None, ALU.mult).then_inc(w_fold, 1)
            dve.wait_ge(w_prod, 3)
            for c in range(C2):
                dve.tensor_scalar(Wvu[:, c], ps_mid[1][:, c * D:(c + 1) * D], col("lnkv_g", c), None,
                                  ALU.mult).then_inc(w_fold, 1)
            dve.wait_ge(w_prod, 4)
            dve.tensor_tensor(ckv[:, 2:4, 0], ps_low[0][:, 1, 0:2], colv[:, COL["bv"]:COL["bv"] + 2],
                              ALU.add).then_inc(w_fold, 1)
            dve.wait_ge(w_fold, FOLD_CV)
            dve.wait_ge(consts, 5)
            for c in range(C2):
                dve.tensor_scalar(bcol[:, c], ones[:], ckv[:, 2 + c], None, ALU.mult).then_inc(cv_spread, 1)
            dve.wait_ge(w_prod, 5)
            for c in range(C2):
                dve.tensor_scalar(kbias[:, c:c + 1], ps_low[1][:, 0, c:c + 1], col("lnq_g", c), LOGIT_SCALE,
                                  ALU.mult, ALU.mult).then_inc(w_fold, 1)
            rows_x(0, 0)
            bn_sum(dve, lnx, 0, 0)
            dve.wait_ge(bu_in, 16)
            dve.wait_ge(w_prod, 6)
            for j in range(J2):
                dve.tensor_tensor(vbias[:, j], ps_low[1][:, 1, 0:D], row("bu"), ALU.add).then_inc(w_fold, 1)
            dve.wait_ge(sig_ready, 1)

            def prologue(b, u, first, last):
                if last is None:
                    rows_c(b + 2, u)
                if first is None:
                    rows_y(b - 2, u)
                if last is None:
                    bn_sum(dve, lnc, b + 2, u)
                if last is None or last < B - 1:
                    rows_x(b + 1, 1 - u)
                if first is None:
                    bn_sum(dve, lni, b - 2, u)
                centre_gain(dve, lnx, b, u, X[:, b], XH[:, b], row("q_logsig"), x_scaled)
                if last is None or last < B - 1:
                    bn_sum(dve, lnx, b + 1, 1 - u)
                dve.wait_ge(low_ready, b + 1)
                if isinstance(b, int) and b == 0:
                    dve.wait_ge(w_fold, FOLD_V)
                dve.tensor_tensor(V[:, b, :, 0:D], ps_low[u][:, 0].rearrange("p (j d) -> p j d", j=J2), vbias[:],
                                  ALU.add).then_inc(low_read, 2)
                dve.wait_ge(lnx.coef, b + 1)
                dve.wait_ge(x_scaled, J2 * b + J2)
                dve.scalar_tensor_tensor(out=Y[:, b, 0], in0=XH[:, b, 0], scalar=lnx.ab[:, u, 0, 0:1],
                                         in1=row("q_mu"), op0=ALU.mult, op1=ALU.add).then_inc(y_half, 1)

            pairs(dve, prologue)

            def w1_fold():
                dve.wait_ge(mlp_in, 16)
                for c in range(C2):
                    dve.tensor_scalar(W1g[:, c], wn[:, W1, c], col("lnm_g", c), None, ALU.mult).then_inc(w_fold, 1)
                dve.wait_ge(w_prod, 7)
                dve.tensor_tensor(b1fold[:], ps_low[0][:, 1, 0:2], colv[:, COL["b1"]:COL["b1"] + 2],
                                  ALU.add).then_inc(w_fold, 1)
                dve.tensor_copy(lnbh[:], colv[:, COL_LNB:COL_LNB + HT]).then_inc(lnb_parts, 1)
                dve.wait_ge(lnb_parts, 1)
                dve.tensor_tensor(lnbl[:], colv[:, COL_LNB:COL_LNB + HT], lnbh[:], ALU.subtract).then_inc(lnb_parts, 1)

            def stats_f(b, u):
                dve.wait_ge(x1_ready, J2 * b + J2)
                bn_rows(dve, lnf, u, X[:, b])
                bn_sum(dve, lnf, b, u)

            def apply_f(b, u):
                dve.wait_ge(lnf.coef, b + 1)
                if not early(b):
                    dve.wait_ge(t_ready, b + (T_FFN - 1))
                for j in range(J2):
                    dve.tensor_scalar(XR[:, u, j], X[:, b, j], lnf.mv[:, u, j, 0:1], lnf.ab[:, u, 0, j:j + 1],
                                      ALU.subtract, ALU.mult).then_inc(xf_ready, 1)

            def low_parts(b, u):
                dve.wait_ge(xth_ready, b + 1)
                if not early(b):
                    dve.wait_ge(f1_ready, 4 * b - 4)
                dve.tensor_tensor(XTl[:, u].rearrange("p c k -> p (c k)"), ps_t[0][:],
                                  XTh[:, u].rearrange("p c k -> p (c k)"), ALU.subtract).then_inc(xtl_ready, 1)

            def centre(r, rt):
                dve.wait_ge(gelu_done, 2 * r + 2)
                if not early(r):
                    dve.wait_ge(sq_done, 2 * r - 2)
                dve.tensor_scalar(gneg[:, rt:rt + 1], gsum[:, rt, 0:1], gsum[:, rt, 1:2], -1.0 / H,
                                  ALU.add, ALU.mult).then_inc(gneg_ready, 1)
                if not early(r):
                    dve.wait_ge(tg_ready, 2 * r - 2)
                dve.wait_ge(gneg_ready, r + 1)
                for h in range(2):
                    dve.scalar_tensor_tensor(out=GC[:, rt, h * HALF:(h + 1) * HALF],
                                             in0=Gf[:, rt, h * HALF:(h + 1) * HALF], scalar=gneg[:, rt:rt + 1],
                                             in1=rowv[:, ROW_LNW + h * HALF:ROW_LNW + (h + 1) * HALF],
                                             op0=ALU.add, op1=ALU.mult).then_inc(gc_done, 1)

            def low_half(r, rt, h):
                dve.wait_ge(gth_ready, 2 * r + (h + 1))
                if not early(r):
                    dve.wait_ge(o_ready, r - 1)
                dve.tensor_tensor(GTl[:, rt, 4 * h:4 * h + 4].rearrange("p t k -> p (t k)"), ps_low[rt][:, h],
                                  GTh[:, rt, 4 * h:4 * h + 4].rearrange("p t k -> p (t k)"), ALU.subtract)\
                   .then_inc(gtl_ready, 1)

            def result(b, r, rt, ps=ps_t[1]):
                dve.wait_ge(o_ready, r + 1)
                dve.wait_ge(grstd_ready, r + 1)
                dve.wait_ge(x1_shifted, b + 1)
                dve.scalar_tensor_tensor(out=X[:, b, rt], in0=ps[:, 0:D], scalar=grstd[:, rt, 2:3],
                                         in1=X[:, b, rt], op0=ALU.mult, op1=ALU.add).then_inc(o_done, 1)

            def ffn(b, u, rt, last=None):
                r = 2 * b + rt
                first = isinstance(b, int) and b == 0
                if rt == 0 and last is None:
                    stats_f(b + 2, u)
                centre(r, rt)
                if not first:
                    result(b - 1, r - 2, rt)
                if rt == 1 or not first:
                    low_half(r - 1, 1 - rt, 0)
                    low_half(r - 1, 1 - rt, 1)
                if rt == 0 and (last is None or last < B - 1):
                    low_parts(b + 1, 1 - u)
                if rt == 1 and last is None:
                    apply_f(b + 2, u)

            def into_ffn(s):
                for b in range(2 * (s - LEAD), min(2 * (s - LEAD) + 2, B)):
                    for j in range(J2):
                        dve.tensor_tensor(X[:, b, j], X[:, b, j], row("lnp_b"), ALU.add).then_inc(x_shifted, 1)
                if s == STEPS - 4:
                    dve.wait_ge(lnb_prod, 1)
                    dve.tensor_copy(lnb_row[0:1, :], ps_low[0][0:1, 1, 0:D]).then_inc(lnb_copied, 1)
                if s == STEPS - 2:
                    dve.wait_ge(lnb_prod, 2)
                    for j in range(J2):
                        dve.tensor_copy(lnb_out[:, j], ps_low[0][:, 1, D:2 * D]).then_inc(lnb_copied, 1)
                if s in (STEPS - 3, STEPS - 1):
                    k = (s - STEPS + 3) // 2
                    stats_f(k, k)
                if s in (STEPS - 2, STEPS):
                    k = (s - STEPS + 2) // 2
                    apply_f(k, k)
                if s == STEPS - 1:
                    low_parts(0, 0)
                if s in (FFN_STEP, FFN_STEP + 1):
                    ffn(0, 0, s - FFN_STEP)

            def gain(it):
                if it and it[1] == 1:
                    r, half, b = it
                    dve.wait_ge(xp_ready, r * B + (b + 1))
                    for j in range(J2):
                        dve.tensor_tensor(XH[:, b, j], XH[:, b, j], row("lnp_g"), ALU.mult).then_inc(p_scaled, 1)

            def ternary_below(t, k):
                cut = bass.ds((t * B + k) * CHUNK, CHUNK)
                dve.tensor_scalar(below[:, k % 2], wf[:, cut], thr[:, 1, bass.ds(t, 1)], None,
                                  ALU.is_lt).then_inc(below_ready, 1)

            def ternary_above(t, k):
                cut = bass.ds((t * B + k) * CHUNK, CHUNK)
                dve.wait_ge(below_ready, t * B + (k + 1))
                dve.scalar_tensor_tensor(out=w3[:, cut], in0=wf[:, cut], scalar=thr[:, 0, bass.ds(t, 1)],
                                         in1=below[:, k % 2], op0=ALU.is_gt, op1=ALU.subtract).then_inc(tern_ready, 1)

            def rounds(t, s, last):
                head = isinstance(t, int) and not last
                at_q = item(t, s, -2, last)
                at_q = at_q if at_q and at_q[1] == 0 and s + 2 >= STEPS else None
                def sum_q():
                    if at_q:
                        bn_sum(dve, lnq, (at_q[0] - 1) * B + at_q[2], at_q[2])

                it3 = item(t, s, 3, last)
                fill = it3 and it3[1] == 0
                if head and s < 2:
                    rows_y(B - 2 + s, s)
                    bn_sum(dve, lni, B - 2 + s, s)
                if it := item(t, s, 2, last):
                    r, half, b = it
                    if half == 0:
                        dve.wait_ge(mid_read, ring(r, half, b) * 2 + (2 + 2 * RING))
                        dve.reciprocal(rinv[:, b], rsum[:, b]).then_inc(rinv_ready, 1)
                if not last:
                    gain(item(t, s, 5, last))
                if it := item(t, s, 2, last):
                    r, half, b = it
                    if half == 0:
                        dve.wait_ge(rinv_ready, r * B + (b + 1))
                        for j in range(J2):
                            dve.tensor_scalar(PR[:, b % 4, j], PR[:, b % 4, j], rinv[:, b, j:j + 1], EPS_ATTN,
                                              ALU.mult, ALU.add).then_inc(attn_ready, 1)
                if at_q:
                    r, half, b = at_q
                    dve.wait_ge(y_ready, r * (J2 * B) + (J2 * b + J2))
                    bn_rows(dve, lnq, b, Y[:, b])
                if it := item(t, s, 1, last):
                    r, half, b = it
                    if half == 0:
                        dve.wait_ge(mid_ready, ring(r, half, b) + (1 + RING))
                        dve.tensor_reduce(nmax[:, b], ps_mid[b % 2][:].rearrange("p (j k) -> p j k", j=J2), AX.X,
                                          ALU.max, negate=True).then_inc(max_ready, 1)
                if at_q and not fill:
                    sum_q()
                chunk = None
                if not head and not last and s < LEAD + B:
                    k = s - LEAD
                    chunk = (t, k)

                if it := item(t, s, 3, last):
                    r, half, b = it
                    n = ring(r, half, b)
                    ps = ps_low[b % 2]
                    dve.wait_ge(low_ready, n + 1)
                    if half == 0:
                        dve.reciprocal(cinv[:, b], ps[:, :, D:D + 1]).then_inc(cinv_ready, 1)
                        sum_q()
                        if chunk is not None:
                            ternary_below(*chunk)
                        dve.wait_ge(cinv_ready, r * B + (b + 1))
                        for j in range(J2):
                            dve.scalar_tensor_tensor(out=S[:, b, j], in0=ps[:, j, 0:D], scalar=cinv[:, b, j],
                                                     in1=Y[:, b, j], op0=ALU.mult, op1=ALU.add).then_inc(low_read, 1)
                        ln = lnm
                    else:
                        dve.wait_ge(s_shifted, r * (J2 * B) + (J2 * b + J2))
                        dve.tensor_tensor(flat(S, b), ps[:, 0], flat(S, b), ALU.add).then_inc(low_read, 2)
                        if chunk is not None:
                            ternary_below(*chunk)
                        ln = lnp
                    dve.wait_ge(low_read, 2 * n + (2 + 2 * RING))
                    bn_rows(dve, ln, b, S[:, b])
                    if chunk is not None:
                        ternary_above(*chunk)
                    bn_sum(dve, ln, r * B + b, b)
                if head and s == SUM_STEP:
                    dve.tensor_scalar(thr[:, 0], ps_low[0][:, 1, D + 2:D + 4], 1.0 / (H * D), EPS_TERNARY,
                                      ALU.mult, ALU.add).then_inc(thr_ready, 1)
                    dve.wait_ge(thr_ready, 1)
                    dve.tensor_scalar(thr[:, 1], thr[:, 0], -0.5, None, ALU.mult).then_inc(thr_ready, 1)
                    dve.wait_ge(thr_ready, 2)
                    dve.tensor_scalar(thr[:, 0], thr[:, 1], -1.0, None, ALU.mult).then_inc(thr_ready, 1)
                    dve.wait_ge(thr_ready, 3)
                if head and s == 1:
                    w1_fold()
                if last:
                    gain(item(t, s, 4, last))
                    into_ffn(s)

            in_rounds(dve, rounds)

            def both(b, u, first, last):
                ffn(b, u, 0, last)
                ffn(b, u, 1, last)

            pairs(dve, both, start=1)
            for h in range(2):
                low_half(2 * B - 1, 1, h)
            result(B - 1, 2 * B - 2, 0)
            result(B - 1, 2 * B - 1, 1, ps_t[0])

        @block.tensor
        def _(pe):
            pe.sem_inc(mid_ready, RING)
            def column(dst, w, v):
                for m in range(C2):
                    for c in range(C2):
                        last = pe.matmul(dst[:, m:m + 1], w[:, c, m * P:(m + 1) * P], v(c),
                                         start=(c == 0), stop=(c == C2 - 1))
                return last

            def context_t(b, u):
                pe.wait_ge(xc_ready, b + 1)
                pe.wait_ge(t_copied, b + 1)
                blocks_t(pe, ps_t[u], XR[:, u])

            pe.wait_ge(consts, 2)
            for _ in range(WARM_UP):
                pe.matmul(ps_t[1][:, 0:P], ones[:], ones[:], start=True, stop=True)
            pe.wait_ge(wkq_in, 16)
            product(pe, side(ps_mid[0]), wt[:, TK], wt[:, TQ]).then_inc(w_prod, 1)
            pe.wait_ge(cols_in, 16)
            pe.wait_ge(wk_in, 16)
            column(ps_low[0][:, 0], wn[:, WK], lambda c: col("lnkv_b", c)).then_inc(w_prod, 1)
            pe.wait_ge(wvu_in, 32)
            product(pe, side(ps_mid[1]), wt[:, TV], wn[:, WU]).then_inc(w_prod, 1)
            column(ps_low[0][:, 1], wn[:, WV], lambda c: col("lnkv_b", c)).then_inc(w_prod, 1)
            pe.wait_ge(consts, 5)
            context_t(0, 0)
            pe.wait_ge(w_fold, FOLD_CK)
            column(ps_low[1][:, 0], wt[:, TQ], lambda c: ckv[:, c]).then_inc(w_prod, 1)
            pe.wait_ge(cv_spread, 2)
            for c in range(C2):
                last = pe.matmul(ps_low[1][:, 1, 0:D], bcol[:, c], wn[:, WU, c], start=(c == 0), stop=(c == C2 - 1))
            last.then_inc(w_prod, 1)

            def keys_values(b, u):
                pe.wait_ge(t_copied, b + (1 + RING))
                if isinstance(b, int) and b == 0:
                    pe.wait_ge(w_fold, FOLD_V)
                pe.wait_ge(low_read, 2 * b + 2)
                product(pe, side(ps_low[u][:, 0]), XT[:, u], Wvu).then_inc(low_ready, 1)
                pe.wait_ge(mid_read, 2 * b + 2)
                product(pe, side(ps_mid[u]), Wkq, XT[:, u]).then_inc(mid_ready, 1)

            def prologue(b, u, first, last):
                if last is None or last < B - 1:
                    context_t(b + 1, 1 - u)
                keys_values(b, u)

            pairs(pe, prologue)

            pe.wait_ge(mlp_in, 16)
            pe.wait_ge(low_read, 2 * (B - 1) + 2 * RING)
            column(ps_low[0][:, 1], wn[:, W1], lambda c: col("lnm_b", c)).then_inc(w_prod, 1)

            def rows_t(b, u):
                pe.wait_ge(xf_ready, 2 * b + 2)
                if isinstance(b, int) and b == 0:
                    pe.wait_ge(t_copied, T_FFN + RING)
                else:
                    pe.wait_ge(xtl_ready, b)
                blocks_t(pe, ps_t[0], XR[:, u])

            def fc(b, u, r, rt):
                if rt == 0:
                    pe.wait_ge(xtl_ready, b + 1)
                for h in range(2):
                    if isinstance(r, int) and r == 0:
                        pe.wait_ge(mid_read, 2 * T_FFN + 2 * RING)
                    else:
                        pe.wait_ge(gelu_done, 2 * r + (h - 1))
                    parts = [(c, part) for c in range(C2) for part in (XTh, XTl)]
                    for k, (c, part) in enumerate(parts):
                        last = pe.matmul(ps_mid[h][:], part[:, u, c, rt * P:(rt + 1) * P],
                                         WfT[:, c, h * HALF:(h + 1) * HALF], start=(k == 0), stop=(k == 3))
                    last.then_inc(f1_ready, 1)

            def hidden_t(r, rt):
                for h in range(2):
                    pe.wait_ge(gc_done, 2 * r + (h + 1))
                    if not early(r):
                        pe.wait_ge(gtl_ready, 2 * r + (h - 3))
                    elif h == 0:
                        pe.wait_ge(low_read, 2 * (T_FFN - 1 + r) + 2 * RING)
                    elif r == 0:
                        pe.wait_ge(lnb_copied, 3)
                    for k in range(4):
                        last = pe.transpose(ps_low[rt][:, h, k * P:(k + 1) * P],
                                            GC[:, rt, (4 * h + k) * P:(4 * h + k + 1) * P], ident[:])
                    last.then_inc(tg_ready, 1)

            def proj(r, rt, ps=ps_t[1]):
                pe.wait_ge(gtl_ready, 2 * r + 2)
                if ps is ps_t[1] and not (isinstance(r, int) and r == 0):
                    pe.wait_ge(o_done, r)
                for k in range(HT):
                    for part in (GTh, GTl):
                        last = pe.matmul(ps[:, 0:D], part[:, rt, k], WpT[:, k],
                                         start=(k == 0 and part is GTh), stop=(k == HT - 1 and part is GTl))
                last.then_inc(o_ready, 1)

            def ffn(b, u, rt, last=None):
                r = 2 * b + rt
                first = isinstance(b, int) and b == 0
                fc(b, u, r, rt)
                if rt == 1 or not first:
                    hidden_t(r - 1, 1 - rt)
                if rt == 0 and (last is None or last < B - 1):
                    rows_t(b + 1, 1 - u)
                if not first:
                    proj(r - 2, rt)

            def into_ffn(s):
                if s == STEPS - 4:
                    pe.wait_ge(tern_ready, TERN_ALL)
                    pe.wait_ge(lnb_parts, 2)
                    for k in range(HT):
                        for part in (lnbh, lnbl):
                            last = pe.matmul(ps_low[0][0:1, 1, 0:D], part[:, k:k + 1], WpT[:, k],
                                             start=(k == 0 and part is lnbh), stop=(k == HT - 1 and part is lnbl))
                    last.then_inc(lnb_prod, 1)
                if s == STEPS - 3:
                    pe.wait_ge(lnb_copied, 1)
                    pe.matmul(ps_low[0][:, 1, D:2 * D], ones[0:1, :], lnb_row[0:1, :], start=True, stop=True)\
                      .then_inc(lnb_prod, 1)
                if s == STEPS - 1:
                    rows_t(0, 0)
                if s in (FFN_STEP, FFN_STEP + 1):
                    ffn(0, 0, s - FFN_STEP)

            def rounds(t, s, last):
                if it := item(t, s, 0, last):
                    r, half, b = it
                    if half == 0:
                        pe.wait_ge(xq_ready, r * B + (b + 1 + RING))
                    else:
                        pe.wait_ge(xm_ready, r * B + (b + 1))
                    pe.wait_ge(t_copied, ring(r, half, b) + 1)
                    blocks_t(pe, ps_t[b % 2], XH[:, b])
                if it := item(t, s, 1, last):
                    r, half, b = it
                    n = ring(r, half, b)
                    pe.wait_ge(t_copied, n + (1 + RING))
                    pe.wait_ge(mid_read, 2 * n + 2)
                    if half == 0:
                        product(pe, side(ps_mid[b % 2]), KT[:, b], XT[:, b % 2]).then_inc(mid_ready, 1)
                    else:
                        product(pe, side(ps_mid[b % 2]), W1g, XT[:, b % 2]).then_inc(mid_ready, 1)
                if it := item(t, s, 3, last):
                    r, half, b = it
                    n = ring(r, half, b)
                    ps = ps_low[b % 2]
                    if half == 0:
                        pe.wait_ge(attn_ready, r * (J2 * B) + (J2 * b + J2))
                        pe.wait_ge(low_read, 2 * n + 2)
                        if isinstance(t, int) and s == 3 and not last:
                            pe.wait_ge(w_fold, FOLD_ALL)
                        if isinstance(t, int) and s == SUM_STEP and not last:
                            pe.wait_ge(mag_ready, 2)
                            pe.matmul(ps[:, 1, D + 2:D + 4], ones[:], absum[:], start=True, stop=True)
                        product(pe, lambda m: ps[:, m, 0:D + 1], PR[:, b % 4], V[:, b], D + 1).then_inc(low_ready, 1)
                    else:
                        pe.wait_ge(mid_read, 2 * n + (2 + 2 * RING))
                        pe.wait_ge(low_read, 2 * n + 2)
                        product(pe, side(ps[:, 0]), GT[:, b % 4], wn[:, W2]).then_inc(low_ready, 1)
                if last:
                    into_ffn(s)

            in_rounds(pe, rounds)

            def both(b, u, first, last):
                ffn(b, u, 0, last)
                ffn(b, u, 1, last)

            pairs(pe, both, start=1)
            hidden_t(2 * B - 1, 1)
            proj(2 * B - 2, 0)
            proj(2 * B - 1, 1, ps_t[0])


def kernel(**inputs):
    import numpy as np
    import concourse.bacc as bacc
    from concourse.bass_utils import run_bass_kernel_spmd

    g = {k: np.asarray(v) for k, v in inputs.items()}
    xc = {k[len("L0_xcond_"):]: v for k, v in g.items() if k.startswith("L0_xcond_")}

    def tiles(w):
        r, c = w.shape
        return w.reshape(r // P, P, c).transpose(1, 0, 2).reshape(P, -1)

    def columns(v):
        return v.reshape(-1, P).T

    arrays = {
        "x": g["x"],
        "ctx": g["ctx_1024"],
        "w_nat": np.stack([tiles(xc[n]) for n in ("wk", "wv", "wu", "w1", "w2")]),
        "w_tr": np.stack([tiles(xc[n].T) for n in ("wk", "wq", "wv")]),
        "w_fc_t": tiles(g["L0_ffn_W_fc"].T),
        "w_proj_t": tiles(g["L0_ffn_W_proj"].T),
        "cols": np.concatenate([columns(xc[n]) for n in COL] + [columns(g["L0_ffn_ln_b"])], axis=1),
        "rows": np.concatenate([xc[n].reshape(-1) for n in ROW] + [g["L0_ffn_ln_w"], g["cond_1024"].reshape(-1)]),
    }
    arrays = {k: np.ascontiguousarray(v) for k, v in arrays.items()}
    nc = bacc.Bacc("TRN2", target_bir_lowering=False, num_devices=1)
    aps = [nc.dram_tensor(k, v.shape, mybir.dt.from_np(v.dtype), kind="ExternalInput").ap() for k, v in arrays.items()]
    out = nc.dram_tensor("out", g["x"].shape, F32, kind="ExternalOutput").ap()
    build(nc, *aps, out)
    r = run_bass_kernel_spmd(nc, [arrays], core_ids=[0])
    return r.results[0]["out"]
```
